# Optimizing a Trainium2 kernel written in Bass

```python
import numpy as np
import jax
import jax.numpy as jnp

def _softmax(x, axis=-1):
    return jax.nn.softmax(x, axis=axis)

def _gelu(x):
    return jax.nn.gelu(x, approximate=True)

def _silu(x):
    return jax.nn.silu(x)

def _sigmoid(x):
    return jax.nn.sigmoid(x)

def _layernorm(x, axis=-1, eps=1e-05):
    m = jnp.mean(x, axis=axis, keepdims=True)
    v = jnp.var(x, axis=axis, keepdims=True)
    return (x - m) / jnp.sqrt(v + eps)

def _scatter_add(tgt, idx, src, axis=0):
    return tgt.at[idx].add(src)

def _segment_sum(src, seg, n):
    return jax.ops.segment_sum(src, seg, n)
kernel_name = 'mk_gnn_resnorm_d4_gnn_r32_e98fc3'

def setup_inputs(seed: int=0):
    np.random.seed(seed)
    _w = jnp.asarray

    def _rec_inputs():
        import jax
        import jax.numpy as jnp
        _gk = jax.random.key(seed)
        x = -0.000202 + 1 * jax.random.normal(jax.random.fold_in(_gk, 1), (50000, 128), jnp.float32)
        src = jax.random.randint(jax.random.fold_in(_gk, 2), (25000,), 0, 50000, jnp.int32)
        dst = jax.random.randint(jax.random.fold_in(_gk, 3), (25000,), 0, 50000, jnp.int32)
        _o = jnp.argsort(dst, stable=True)
        src = src[_o]
        dst = dst[_o]
        edge_weight = jax.random.uniform(jax.random.fold_in(_gk, 13), (25000,), jnp.float32, 0.0, 1)
        return (x, src, dst, edge_weight)
    x, src, dst, edge_weight = _rec_inputs()

    def _L0_gnn_setup():
        import jax, jax.numpy as jnp
        import numpy as np
        N_NODES = 50000
        N_EDGES = 25000
        HID = 128
        key = jax.random.key(seed)
        ks = jax.random.split(key, 10)
        s_msg = 1.0 / np.sqrt(2 * HID + 1)
        s_u1 = 1.0 / np.sqrt(2 * HID)
        s_u2 = 1.0 / np.sqrt(HID)
        return {'z': jax.random.normal(ks[0], (N_NODES, HID), dtype=jnp.float32), 'edge_weight': jax.random.uniform(ks[1], (N_EDGES,), dtype=jnp.float32), 'edge_src': jax.random.randint(ks[2], (N_EDGES,), 0, N_NODES), 'edge_dst': jax.random.randint(ks[3], (N_EDGES,), 0, N_NODES), 'Wm': jax.random.normal(ks[4], (2 * HID + 1, HID), dtype=jnp.float32) * s_msg, 'bm': jax.random.normal(ks[5], (HID,), dtype=jnp.float32) * s_msg, 'W1': jax.random.normal(ks[6], (2 * HID, HID), dtype=jnp.float32) * s_u1, 'b1': jax.random.normal(ks[7], (HID,), dtype=jnp.float32) * s_u1, 'W2': jax.random.normal(ks[8], (HID, HID), dtype=jnp.float32) * s_u2, 'b2': jax.random.normal(ks[9], (HID,), dtype=jnp.float32) * s_u2}
    _L0_gnn_all = _L0_gnn_setup()
    _L0_gnn_in = {k: v for k, v in _L0_gnn_all.items() if k in ('Wm', 'bm', 'W1', 'b1', 'W2', 'b2')}
    del _L0_gnn_all

    def _L1_gnn_setup():
        import jax, jax.numpy as jnp
        import numpy as np
        N_NODES = 50000
        N_EDGES = 25000
        DIM = 128
        N_LAYERS = 3
        NEG_SLOPE = 0.2
        key = jax.random.key(seed)
        ks = jax.random.split(key, 6)
        scale = 1.0 / np.sqrt(DIM)
        return {'node_features': jax.random.normal(ks[0], (N_NODES, DIM), dtype=jnp.float32), 'edge_index': jax.random.randint(ks[1], (2, N_EDGES), 0, N_NODES, dtype=jnp.int64), 'W_src': jax.random.normal(ks[2], (N_LAYERS, DIM, DIM), dtype=jnp.float32) * scale, 'W_dst': jax.random.normal(ks[3], (N_LAYERS, DIM, DIM), dtype=jnp.float32) * scale, 'att': jax.random.normal(ks[4], (N_LAYERS, DIM), dtype=jnp.float32) * scale, 'bias': jnp.zeros((N_LAYERS, DIM), dtype=jnp.float32)}
    _L1_gnn_all = _L1_gnn_setup()
    _L1_gnn_in = {k: v for k, v in _L1_gnn_all.items() if k in ('W_src', 'W_dst', 'att', 'bias')}
    del _L1_gnn_all

    def _L2_gnn_setup():
        import jax, jax.numpy as jnp
        import numpy as np
        N_NODES = 3125
        N_EDGES = 50000
        C_IN = 128
        C_OUT = 128
        key = jax.random.key(seed)
        k1, k2, k3, k4, k5 = jax.random.split(key, 5)
        x = jax.random.normal(k1, (N_NODES, C_IN), dtype=jnp.float32)
        edge_src = jax.random.randint(k2, (N_EDGES,), 0, N_NODES, dtype=jnp.int32)
        edge_dst = jax.random.randint(k3, (N_EDGES,), 0, N_NODES, dtype=jnp.int32)
        weight = jax.random.normal(k4, (C_OUT, 2 * C_IN), dtype=jnp.float32) * 0.05
        bias = jax.random.normal(k5, (C_OUT,), dtype=jnp.float32) * 0.05
        return {'x': x, 'edge_src': edge_src, 'edge_dst': edge_dst, 'weight': weight, 'bias': bias}
    _L2_gnn_all = _L2_gnn_setup()
    _L2_gnn_in = {k: v for k, v in _L2_gnn_all.items() if k in ('weight', 'bias')}
    del _L2_gnn_all

    def _L3_gnn_setup():
        import jax, jax.numpy as jnp
        import numpy as np
        NEG_SLOPE = 0.2

        def gat_conv(x, src, dst, n, W, att_src, att_dst, bias, concat):
            H, C = att_src.shape
            xp = (x @ W).reshape(n, H, C)
            a_src = jnp.einsum('nhc,hc->nh', xp, att_src)
            a_dst = jnp.einsum('nhc,hc->nh', xp, att_dst)
            e = jax.nn.leaky_relu(a_src[src] + a_dst[dst], NEG_SLOPE)
            m = jax.ops.segment_max(e, dst, num_segments=n)
            ex = jnp.exp(e - m[dst])
            s = jax.ops.segment_sum(ex, dst, num_segments=n)
            alpha = ex / s[dst]
            out = jax.ops.segment_sum(xp[src] * alpha[:, :, None], dst, num_segments=n)
            out = out.reshape(n, H * C) if concat else out.mean(axis=1)
            return out + bias
        key = jax.random.key(seed)
        ks = jax.random.split(key, 16)
        N, E, D, H = (3125, 50000, 128, 4)
        HID, OUT = (128, 128)
        C = HID // H
        x = jax.random.normal(ks[0], (N, D), dtype=jnp.float32)
        edge_index = jax.random.randint(ks[1], (2, E), 0, N, dtype=jnp.int32)
        g = lambda k, shp: jax.random.normal(k, shp, dtype=jnp.float32) * 0.1
        return {'x': x, 'edge_index': edge_index, 'W1': g(ks[2], (D, H * C)), 'as1': g(ks[3], (H, C)), 'ad1': g(ks[4], (H, C)), 'b1': jnp.zeros((H * C,), jnp.float32), 'W2': g(ks[5], (HID, H * C)), 'as2': g(ks[6], (H, C)), 'ad2': g(ks[7], (H, C)), 'b2': jnp.zeros((H * C,), jnp.float32), 'W3': g(ks[8], (HID, H * OUT)), 'as3': g(ks[9], (H, OUT)), 'ad3': g(ks[10], (H, OUT)), 'b3': jnp.zeros((OUT,), jnp.float32)}
    _L3_gnn_all = _L3_gnn_setup()
    _L3_gnn_in = {k: v for k, v in _L3_gnn_all.items() if k in ('W1', 'as1', 'ad1', 'b1', 'W2', 'as2', 'ad2', 'b2', 'W3', 'as3', 'ad3', 'b3')}
    del _L3_gnn_all
    return {'x': x, 'src': src, 'dst': dst, 'edge_weight': edge_weight, 'L0_gnn_Wm': _L0_gnn_in['Wm'], 'L0_gnn_bm': _L0_gnn_in['bm'], 'L0_gnn_W1': _L0_gnn_in['W1'], 'L0_gnn_b1': _L0_gnn_in['b1'], 'L0_gnn_W2': _L0_gnn_in['W2'], 'L0_gnn_b2': _L0_gnn_in['b2'], 'L1_gnn_W_src': _L1_gnn_in['W_src'], 'L1_gnn_W_dst': _L1_gnn_in['W_dst'], 'L1_gnn_att': _L1_gnn_in['att'], 'L1_gnn_bias': _L1_gnn_in['bias'], 'L2_gnn_weight': _L2_gnn_in['weight'], 'L2_gnn_bias': _L2_gnn_in['bias'], 'L3_gnn_W1': _L3_gnn_in['W1'], 'L3_gnn_as1': _L3_gnn_in['as1'], 'L3_gnn_ad1': _L3_gnn_in['ad1'], 'L3_gnn_b1': _L3_gnn_in['b1'], 'L3_gnn_W2': _L3_gnn_in['W2'], 'L3_gnn_as2': _L3_gnn_in['as2'], 'L3_gnn_ad2': _L3_gnn_in['ad2'], 'L3_gnn_b2': _L3_gnn_in['b2'], 'L3_gnn_W3': _L3_gnn_in['W3'], 'L3_gnn_as3': _L3_gnn_in['as3'], 'L3_gnn_ad3': _L3_gnn_in['ad3'], 'L3_gnn_b3': _L3_gnn_in['b3']}

def reference(x, src, dst, edge_weight, L0_gnn_Wm, L0_gnn_bm, L0_gnn_W1, L0_gnn_b1, L0_gnn_W2, L0_gnn_b2, L1_gnn_W_src, L1_gnn_W_dst, L1_gnn_att, L1_gnn_bias, L2_gnn_weight, L2_gnn_bias, L3_gnn_W1, L3_gnn_as1, L3_gnn_ad1, L3_gnn_b1, L3_gnn_W2, L3_gnn_as2, L3_gnn_ad2, L3_gnn_b2, L3_gnn_W3, L3_gnn_as3, L3_gnn_ad3, L3_gnn_b3):
    import jax
    import jax.numpy as jnp

    def _L0_gnn_ref(z, edge_weight, edge_src, edge_dst, Wm, bm, W1, b1, W2, b2):
        import jax, jax.numpy as jnp
        import numpy as np
        N_NODES = 50000
        N_EDGES = 25000
        HID = 128
        n, H = z.shape
        Wd, Ws, ww = (Wm[:H], Wm[H:2 * H], Wm[2 * H])
        msgs = z[edge_dst] @ Wd + z[edge_src] @ Ws + edge_weight[:, None] * ww[None, :] + bm
        agg = jax.ops.segment_max(msgs, edge_dst, num_segments=n)
        deg = jax.ops.segment_sum(jnp.ones_like(edge_weight), edge_dst, num_segments=n)
        agg = jnp.where(deg[:, None] > 0, agg, jnp.zeros((), dtype=z.dtype))
        W1a, W1b = (W1[:H], W1[H:])
        hidden = jax.nn.relu(z @ W1a + agg @ W1b + b1)
        return hidden @ W2 + b2

    def _L1_gnn_ref(node_features, edge_index, W_src, W_dst, att, bias):
        import jax, jax.numpy as jnp
        import numpy as np
        N_NODES = 50000
        N_EDGES = 25000
        DIM = 128
        N_LAYERS = 3
        NEG_SLOPE = 0.2
        N = node_features.shape[0]
        loops = jnp.arange(N, dtype=edge_index.dtype)
        ei = jnp.concatenate([edge_index, jnp.stack([loops, loops])], axis=1)
        src, dst = (ei[0], ei[1])
        x = node_features
        for l in range(W_src.shape[0]):
            xs = x @ W_src[l]
            xd = x @ W_dst[l]
            h = jax.nn.leaky_relu(xs[src] + xd[dst], negative_slope=NEG_SLOPE)
            e = h @ att[l]
            m = jax.ops.segment_max(e, dst, num_segments=N)
            a = jnp.exp(e - m[dst])
            s = jax.ops.segment_sum(a, dst, num_segments=N)
            alpha = a / (s[dst] + 1e-16)
            out = jax.ops.segment_sum(alpha[:, None] * xs[src], dst, num_segments=N) + bias[l]
            x = jax.nn.relu(out)
        return x

    def _L2_gnn_ref(x, edge_src, edge_dst, weight, bias):
        import jax, jax.numpy as jnp
        import numpy as np
        N_NODES = 3125
        N_EDGES = 50000
        C_IN = 128
        C_OUT = 128
        n = x.shape[0]
        agg = jax.ops.segment_sum(x[edge_src], edge_dst, num_segments=n)
        deg = jax.ops.segment_sum(jnp.ones_like(edge_dst, dtype=x.dtype), edge_dst, num_segments=n)
        inv_w = jnp.where(deg > 0, 1.0 / jnp.maximum(deg, 1.0), 0.0)
        h = agg * inv_w[:, None]
        h = jnp.concatenate([h, x], axis=-1)
        return h @ weight.T + bias

    def _L3_gnn_ref(x, edge_index, W1, as1, ad1, b1, W2, as2, ad2, b2, W3, as3, ad3, b3):
        import jax, jax.numpy as jnp
        import numpy as np
        NEG_SLOPE = 0.2

        def gat_conv(x, src, dst, n, W, att_src, att_dst, bias, concat):
            H, C = att_src.shape
            xp = (x @ W).reshape(n, H, C)
            a_src = jnp.einsum('nhc,hc->nh', xp, att_src)
            a_dst = jnp.einsum('nhc,hc->nh', xp, att_dst)
            e = jax.nn.leaky_relu(a_src[src] + a_dst[dst], NEG_SLOPE)
            m = jax.ops.segment_max(e, dst, num_segments=n)
            ex = jnp.exp(e - m[dst])
            s = jax.ops.segment_sum(ex, dst, num_segments=n)
            alpha = ex / s[dst]
            out = jax.ops.segment_sum(xp[src] * alpha[:, :, None], dst, num_segments=n)
            out = out.reshape(n, H * C) if concat else out.mean(axis=1)
            return out + bias
        n = x.shape[0]
        loops = jnp.arange(n, dtype=edge_index.dtype)
        src = jnp.concatenate([edge_index[0], loops])
        dst = jnp.concatenate([edge_index[1], loops])
        h = jax.nn.relu(gat_conv(x, src, dst, n, W1, as1, ad1, b1, True))
        h = jax.nn.relu(gat_conv(h, src, dst, n, W2, as2, ad2, b2, True))
        return gat_conv(h, src, dst, n, W3, as3, ad3, b3, False)
    edge_index = jnp.stack([src, dst])
    x = _layernorm(x + _L0_gnn_ref(x, edge_weight, src, dst, L0_gnn_Wm, L0_gnn_bm, L0_gnn_W1, L0_gnn_b1, L0_gnn_W2, L0_gnn_b2), axis=-1)
    x = _layernorm(x + _L1_gnn_ref(x, edge_index, L1_gnn_W_src, L1_gnn_W_dst, L1_gnn_att, L1_gnn_bias), axis=-1)
    x = _layernorm(x + _L2_gnn_ref(x, src, dst, L2_gnn_weight, L2_gnn_bias), axis=-1)
    x = _layernorm(x + _L3_gnn_ref(x, edge_index, L3_gnn_W1, L3_gnn_as1, L3_gnn_ad1, L3_gnn_b1, L3_gnn_W2, L3_gnn_as2, L3_gnn_ad2, L3_gnn_b2, L3_gnn_W3, L3_gnn_as3, L3_gnn_ad3, L3_gnn_b3), axis=-1)
    return x

_drawn_inputs = setup_inputs


def setup_inputs(seed=0):
    import zlib

    import numpy as np

    out = dict(_drawn_inputs(seed))
    spreads = {'L1_gnn_bias': (0.0, 0.1),
     'L3_gnn_b1': (0.0, 0.1),
     'L3_gnn_b2': (0.0, 0.1),
     'L3_gnn_b3': (0.0, 0.1)}
    factors = {'edge_weight': 8.0,
     'L0_gnn_bm': 3.269,
     'L1_gnn_W_dst': 8.0,
     'L1_gnn_att': 3.686,
     'L3_gnn_as1': 3.778,
     'L3_gnn_ad1': 8.0,
     'L3_gnn_as2': 8.0,
     'L3_gnn_ad2': 8.0,
     'L3_gnn_as3': 8.0,
     'L3_gnn_ad3': 8.0}
    for name, (base, spread) in spreads.items():
        noise = np.random.default_rng([zlib.crc32(name.encode()), seed]).standard_normal(out[name].shape)
        drawn = base * np.exp(spread * noise) if base else spread * noise
        out[name] = jnp.asarray(drawn.astype(out[name].dtype))
    for name, factor in factors.items():
        out[name] = (out[name] * factor).astype(out[name].dtype)
    return out
```

```python
import concourse.bass as bass
from concourse import mybir
from contextlib import ExitStack

F32 = mybir.dt.float32
I32 = mybir.dt.int32
U8 = mybir.dt.uint8
ALU = mybir.AluOpType
ACT = mybir.ActivationFunctionType

P = 128
N, E = 50000, 25000
CH = 512
TILES = CH // P
DL, EL = 4, 5
NCH = -(-N // (CH * DL)) * DL
ECH = -(-E // (CH * EL)) * EL
NP, EP = NCH * CH, ECH * CH
DIT, EIT = NCH // DL, ECH // EL
NT = EP // P
RP = NT // 2
TAB = NP + EP
HEADS = 4
EPS = 1e-5
SLOPE = 0.2
FAR = float(1 << 20)
NEG = -3.0e38
CREDIT = 2 * EL

ENGINES = 5
TRANSPOSE_ADDS = True
STOP = 99
DEBUG = ()


class Stage:

    def __init__(self, sem):
        self.sem = sem

    def done(self, n):
        return n + (CREDIT + 1)


class Pass:

    def __init__(self, sem, index, count):
        self.sem, self.index, self.per_round = sem, index, count * DL

    def done(self, it, lane):
        return it * self.per_round + (self.per_round + self.index * DL + lane + 1)

    def done_before(self, it, lane):
        return it * self.per_round + (self.index * DL + lane + 1)


def build(nc, a, out, dbg):
    ctx = ExitStack()
    with ctx:
        def sb(name, shape, dt=F32):
            return ctx.enter_context(nc.sbuf_tensor(name, shape, dt))

        def sem(name):
            return ctx.enter_context(nc.semaphore(name))

        def dram(name, shape, dt=F32):
            kind = "ExternalOutput" if name in dbg else "Internal"
            return nc.dram_tensor(name, shape, dt, kind=kind).ap()

        node_row = dram("node_row", [NP, 1], I32)
        table = [None] + [dram(f"table{i}", [TAB, P]) for i in range(1, 8)]
        own = {0: dram("own0", [EP, P]), 1: dram("own1", [EP, P]), 5: dram("own5", [EP, P])}
        staged = dram("staged", [EP, P])
        scores = dram("scores", [2 * HEADS, EP])

        work = sb("work", [P, EP + 4 * EL * CH])
        state = work[:, 0:EP]

        def lane_buffers(at, lanes):
            return [work[:, at + l * CH:at + (l + 1) * CH] for l in range(lanes)]

        G, H, A, B = [lane_buffers(EP + i * EL * CH, EL) for i in range(4)]
        names = "z zb f0 f1 y x1 xs0 xs1 xs2 x4 xb x5 p5 p6 x7 xo".split()
        d = {nm: lane_buffers(i * DL * CH, DL) for i, nm in enumerate(names)}
        assert len(names) * DL * CH <= EP + 4 * EL * CH

        def rows(buf):
            return buf.rearrange("p (j f) -> p j f", j=TILES)

        same = sb("same", [P, EP + 1], U8)
        ident = sb("ident", [P, P])
        one = sb("one", [1, 1])
        gather_row = sb("gather_row", [P, NT], I32)
        src_col = sb("src_col", [P, NT], I32)
        dst_col = sb("dst_col", [P, NT], I32)
        last_row = sb("last_row", [P, NT], I32)
        idx = [sb(f"idx{l}", [P, TILES], I32) for l in range(EL)]
        idx2 = [sb(f"idx2{l}", [P, TILES], I32) for l in range(EL)]
        shared = sb("shared", [P, EL * CH])
        ew = shared[0:1, :]
        alpha = shared[:, 0:NT * HEADS]
        aself = shared[:, NT * HEADS:2 * NT * HEADS]
        alpha4 = alpha[:, :].rearrange("p (t h) -> p t h", h=HEADS)
        aself4 = aself[:, :].rearrange("p (t h) -> p t h", h=HEADS)
        mean_w = sb("mean_w", [P, NT])
        nxt_col = alpha[:, 0:NT].bitcast(I32)
        slot_row = alpha[:, NT:2 * NT].bitcast(I32)
        lastf = alpha[:, 2 * NT:3 * NT]
        mats = {nm: sb(nm, [P, P]) for nm in
                "Wd0 Ws0 W1a W1b W2 Wz gS0 gS1 gS2 gD0 gD1 gD2 gB0 gB1 gB2 Wa Wx V1 V2 q0 q1 q2 q3 V3m".split()}
        c = {nm: sb("c_" + nm, [P, 1]) for nm in "bm b1 bz gb0 gb1 gb2 att0 att1 att2 natt0 natt1 natt2 vb1 vb2".split()}
        bc = {nm: sb("bc_" + nm, [P, P]) for nm in "b2 gb2 l2 b3".split()}
        ww = sb("ww", [1, P])
        asd = {k: sb(f"asd{k}", [P, 2 * HEADS]) for k in (1, 2, 3)}
        src8 = {k: sb(f"src8{k}", [P, 2 * HEADS]) for k in (1, 2, 3)}
        dst8 = {k: sb(f"dst8{k}", [P, 2 * HEADS]) for k in (1, 2, 3)}
        block_mask = sb("block_mask", [P, HEADS])
        st = sb("st", [P, EL, TILES, 6])
        mv = sb("mv", [P, EL, TILES, 2])
        sd = sb("sd", [P, EL, TILES])
        rs = sb("rs", [P, EL, TILES])
        carry = sb("carry", [P, HEADS])
        eps = sb("eps", [P, 1])
        score_rows = [shared[0:2 * HEADS, l * CH:(l + 1) * CH] for l in range(EL)]
        names_r = "cont contb contz contbz pre suf start".split()
        R = {nm: sb("r_" + nm, [RP, 2 * P]) for nm in names_r}
        frow = sb("frow", [1, 2 * NT])
        erow = sb("erow", [1, 2 * NT + 2])
        ccol = sb("ccol", [RP, 4])

        def tmp(i):
            return work[0:RP, EP + i * 2 * P:EP + (i + 1) * 2 * P]

        T = {nm: tmp(i) for i, nm in enumerate("e s d f b t m w c u di dm".split())}
        bank = [ctx.enter_context(nc.psum_tensor(f"bank{i}", [P, CH], F32)) for i in range(8)]


        def stages(text):
            return {nm: Stage(sem(nm)) for nm in text.split()}

        all_stages = []

        def stage_set(prefix, text):
            got = {nm: Stage(sem(prefix + nm)) for nm in text.split()}
            all_stages.extend(got.values())
            return got

        D = {}
        for owner, text in (("tensor", "t0 m0 r0 t1 r1 t2 r2 t3 r3 t4 r4 t5 r5 t6 r6 t7 t8 r7"),
                            ("scalar", "f0 f1 f0b xs0 f1b xs1 f0c xs2 f1c f0d p5 f1d p6 f0e x7"),
                            ("vector", "zb y0 ya y1 xb y2 xb5 y3"), ("rows", "stored")):
            s_pass = sem("dense_" + owner)
            for i, nm in enumerate(text.split()):
                D[nm] = Pass(s_pass, i, len(text.split()))
        LND = stage_set("dn_", "st var sd rs out")
        LNS = stage_set("sn_", "st var sd rs out")
        E0 = stage_set("e_", "gT a hT s m neg scan h r o state")
        GA = stage_set("g_", "idx pre a self b la lb e row stored")
        LA = stage_set("l_", "idx gT a e row stored")
        CA = stage_set("c_", "g h sum t v state")
        CM = stage_set("m_", "idx g t v z state")
        C3 = stage_set("h_", "g h sum t v carry z state")
        TL = stage_set("t_", "s a t b y xt x cp r g idx stored")
        SP_ = stage_set("s_", "s a cp r g stored")
        s_phase = sem("phase")
        s_pool = sem("pool_settled")
        s_dve = sem("vector_settled")
        s_w = sem("weights")
        s_const = sem("const")
        s_set, s_setp, s_seta = sem("setup_vector"), sem("setup_tensor"), sem("setup_scalar")
        s_mask, s_map = sem("mask"), sem("map")
        s_vs, s_ts, s_as, s_ds = sem("seg_vector"), sem("seg_tensor"), sem("seg_scalar"), sem("seg_load")

        def lane_sems(name, lanes):
            return [sem(f"{name}{l}") for l in range(lanes)]

        s_z = lane_sems("z_loaded", DL)
        s_zo = lane_sems("dense_store", DL)
        s_in = lane_sems("load", EL)
        s_in2 = lane_sems("load_own", EL)
        s_ew = lane_sems("edge_weights", EL)
        s_ga = lane_sems("gathered", EL)
        s_gb = lane_sems("gathered_dst", EL)
        s_mk = lane_sems("mask_load", 2)
        s_out = lane_sems("scattered", EL)
        s_dsc, s_sc, s_sc2, s_gr = sem("pool_step"), sem("map_scattered"), sem("map_gathered"), sem("gather_rows")
        s_sync = sem("sync_step")
        s_zg, s_zs = sem("x_gathered"), sem("x_stored")
        s_settle, s_cz = sem("vector_step"), sem("carry_cleared")
        s_st = lane_sems("store", EL)
        block = ctx.enter_context(nc.Block())

        def at(it, lane):
            return it * (EL * CH) + lane * CH

        def at_back(it, lane):
            return (ECH - 1) * CH - lane * CH - it * (EL * CH)

        def num(use, it, lane):
            return use * ECH + it * EL + lane

        def turn(use, it, per=1):
            return (it + (use * EIT + 1)) * (16 * per)

        def slot_rows(tensor, start, base=0):
            return tensor[bass.ds(base + start, CH), :].rearrange("(j p) f -> p j f", p=P)

        phase_no = {}

        def end_phase(eng, last=False):
            phase_no[eng.engine] = phase_no.get(eng.engine, 0) + 1
            eng.drain().then_inc(s_phase, 1)
            if not last:
                eng.wait_ge(s_phase, ENGINES * phase_no[eng.engine])
                eng.nop()

        def settle(eng, s):
            eng.sem_inc(s, 1)

        def transpose4(src, dst, **kw):
            for j in range(TILES):
                ins = nc.tensor.transpose(dst[:, j * P:(j + 1) * P], src[:, j * P:(j + 1) * P], ident[:, :])
            return ins

        def rows4(src, mat, dst):
            for j in range(TILES):
                ins = nc.tensor.matmul(dst[:, j * P:(j + 1) * P], src[:, j * P:(j + 1) * P], mat[:, :],
                                       start=True, stop=True)
            return ins

        tmp_a, tmp_x = work[:, 0:P], work[:, P:2 * P]
        V3 = work[:, 2 * P:2 * P + HEADS * P]
        asc = {k: work[:, 6 * P + 2 * k:6 * P + 2 * k + 2] for k in (1, 2)}
        comb = {k: work[:, 6 * P + 16 + 8 * k:6 * P + 24 + 8 * k] for k in (1, 2, 3)}
        turned = work[:, 7 * P:16 * P]
        tcol = work[:, 16 * P:16 * P + NT]
        MB = EP // 10
        mbuf = [work[:, 4096 + l * 2816:4096 + l * 2816 + MB + 1].bitcast(I32) for l in range(2)]
        node_iota = work[:, 10000:10000 + NP // P].bitcast(I32)
        dR, pR, nR = (tmp(i).bitcast(I32) for i in range(3))

        def compact(v):
            return v.rearrange("(g q i) -> q g i", g=2, i=P)

        def compact_sb(v):
            return v.rearrange("q (g i) -> q g i", g=2)

        def column(v):
            return v.rearrange("(p o) -> p o", o=1)

        loads = [(mats["Wd0"][:, :], a["L0_gnn_Wm"][0:P, :]), (mats["Ws0"][:, :], a["L0_gnn_Wm"][P:2 * P, :]),
                 (ww[:, :], a["L0_gnn_Wm"][2 * P:2 * P + 1, :]),
                 (mats["W1a"][:, :], a["L0_gnn_W1"][0:P, :]), (mats["W1b"][:, :], a["L0_gnn_W1"][P:2 * P, :]),
                 (mats["W2"][:, :], a["L0_gnn_W2"][:, :]),
                 (tmp_a, a["L2_gnn_weight"][:, 0:P]), (tmp_x, a["L2_gnn_weight"][:, P:2 * P]),
                 (mats["V1"][:, :], a["L3_gnn_W1"][:, :]), (mats["V2"][:, :], a["L3_gnn_W2"][:, :]),
                 (V3, a["L3_gnn_W3"][:, :]),
                 (c["bm"][:, :], column(a["L0_gnn_bm"])), (c["b1"][:, :], column(a["L0_gnn_b1"])),
                 (c["vb1"][:, :], column(a["L3_gnn_b1"])), (c["vb2"][:, :], column(a["L3_gnn_b2"]))]
        for l in range(3):
            loads += [(mats[f"gS{l}"][:, :], a["L1_gnn_W_src"][l]), (mats[f"gD{l}"][:, :], a["L1_gnn_W_dst"][l]),
                      (c[f"gb{l}"][:, :], column(a["L1_gnn_bias"][l])), (c[f"att{l}"][:, :], column(a["L1_gnn_att"][l]))]
        for nm, v in (("b2", a["L0_gnn_b2"]), ("gb2", a["L1_gnn_bias"][2]), ("l2", a["L2_gnn_bias"]), ("b3", a["L3_gnn_b3"])):
            loads.append((bc[nm][:, :], v.partition_broadcast(P)))
        for k in (1, 2):
            loads += [(asc[k][:, 0:1], a[f"L3_gnn_as{k}"].rearrange("h (c o) -> (h c) o", o=1)),
                      (asc[k][:, 1:2], a[f"L3_gnn_ad{k}"].rearrange("h (c o) -> (h c) o", o=1))]
        loads += [(asd[3][:, 0:HEADS], a["L3_gnn_as3"].rearrange("h c -> c h")),
                  (asd[3][:, HEADS:], a["L3_gnn_ad3"].rearrange("h c -> c h"))]
        col_loads = [(src_col[:, :], a["src_col"]), (dst_col[:, :], a["dst_col"]), (nxt_col, a["nxt_col"]),
                     (compact_sb(dR), compact(a["dst_all"][1:1 + EP])), (compact_sb(pR), compact(a["dst_all"][0:EP])),
                     (compact_sb(nR), compact(a["dst_all"][2:2 + EP]))]
        mask_stage = Stage(s_mask)

        def setup_sync(sp):
            for dst, src in col_loads:
                sp.dma_start(dst, src).then_inc(s_const, 16)
            with nc.allow_non_contiguous_dma(reason="1024 elements of the last layer's attention vectors"):
                for dst, src in loads:
                    sp.dma_start(dst, src).then_inc(s_w, 16)
            with sp.Fori(0, 5) as it:
                for l in range(2):
                    sp.wait_ge(s_mask, mask_stage.done(it * 2 + l) - 2)
                    settle(sp, s_sync)
                    sp.dma_start(mbuf[l], a["dst_all"][bass.ds(it * (2 * MB) + l * MB, MB + 1)].partition_broadcast(P))\
                      .then_inc(s_mk[l], 16)

        SETUP = "blk0 blk1 mats turned lin fused last node rowmask frow".split()

        def chain(eng, s):
            n = [0]

            def link(ins):
                n[0] += 1
                ins.then_inc(s, 1)
                eng.wait_ge(s, n[0])
            return link

        def setup_vector(dve):
            v = nc.vector
            link = chain(dve, s_dve)
            dve.sem_inc(s_mask, CREDIT)
            for stage in all_stages:
                dve.sem_inc(stage.sem, CREDIT)
            for nm in ("t0", "f0", "zb", "stored"):
                dve.sem_inc(D[nm].sem, D[nm].per_round)
            link(v.memset(same[:, EP:EP + 1], 0))
            link(v.memset(one[:, :], 1.0))
            link(v.memset(eps[:, :], EPS))
            link(v.memset(block_mask[:, :], 0.0))
            link(v.memset(erow[:, :], 0.0))
            for h in range(HEADS):
                link(v.memset(block_mask[32 * h:32 * h + 32, h:h + 1], 1.0))
            for k in (1, 2, 3):
                link(v.memset(src8[k][:, :], 0.0))
            dve.wait_ge(s_const, 16 * len(col_loads))
            link(v.tensor_tensor(lastf, dst_col[:, :], nxt_col, ALU.not_equal))
            link(v.scalar_tensor_tensor(tcol, dst_col[:, :], FAR, lastf, ALU.subtract, ALU.mult))
            link(v.tensor_scalar(last_row[:, :], tcol, FAR, None, ALU.add))
            v.tensor_copy(tcol[:, 0:1], tcol[:, 1:2]).then_inc(s_map, 1)
            link(v.tensor_tensor(R["cont"][:, :], dR, pR, ALU.is_equal))
            link(v.tensor_tensor(R["contb"][:, :], dR, nR, ALU.is_equal))
            link(v.tensor_scalar(R["start"][:, :], R["cont"][:, :], -1.0, 1.0, ALU.mult, ALU.add))
            link(v.tensor_copy(R["contz"][:, :], R["cont"][:, :]))
            link(v.tensor_copy(R["contbz"][:, :], R["contb"][:, :]))
            for g in range(2):
                link(v.memset(R["contz"][:, g * P:g * P + 1], 0.0))
                link(v.memset(R["contbz"][:, g * P + P - 1:g * P + P], 0.0))
                cg, bg = R["cont"][:, g * P:(g + 1) * P], R["contb"][:, g * P:(g + 1) * P]
                link(v.tensor_tensor_scan(R["pre"][:, g * P:(g + 1) * P], cg, cg, 1.0, ALU.min, ALU.min))
                link(v.tensor_tensor_scan(R["suf"][:, g * P:(g + 1) * P][:, ::-1], bg[:, ::-1], bg[:, ::-1], 1.0,
                                          ALU.min, ALU.min))
            v.tensor_copy(tcol[:, 0:1], tcol[:, 1:2]).then_inc(s_set, 1)
            dve.wait_ge(s_w, 16 * len(loads))
            for k in (1, 2):
                link(v.tensor_scalar(asd[k][:, 0:HEADS], block_mask[:, :], asc[k][:, 0:1], None, ALU.mult))
                link(v.tensor_scalar(asd[k][:, HEADS:], block_mask[:, :], asc[k][:, 1:2], None, ALU.mult))
                link(v.tensor_copy(src8[k][:, 0:HEADS], asd[k][:, 0:HEADS]))
            for k in (1, 2, 3):
                link(v.tensor_copy(comb[k][:, 0:HEADS], asd[k][:, HEADS:]))
                link(v.tensor_tensor(comb[k][:, HEADS:], asd[k][:, 0:HEADS], asd[k][:, HEADS:], ALU.add))
            for l in range(3):
                link(v.tensor_tensor(mats[f"gB{l}"][:, :], mats[f"gS{l}"][:, :], mats[f"gD{l}"][:, :], ALU.add))
                link(v.tensor_scalar(c[f"natt{l}"][:, :], c[f"att{l}"][:, :], -1.0, None, ALU.mult))
            for h in range(HEADS):
                link(v.tensor_scalar(mats[f"q{h}"][:, :], V3[:, h * P:(h + 1) * P], 1.0 / HEADS, None, ALU.mult))
            link(v.tensor_tensor(mats["V3m"][:, :], mats["q0"][:, :], mats["q1"][:, :], ALU.add))
            link(v.tensor_tensor(mats["V3m"][:, :], mats["V3m"][:, :], mats["q2"][:, :], ALU.add))
            link(v.tensor_tensor(mats["V3m"][:, :], mats["V3m"][:, :], mats["q3"][:, :], ALU.add))
            dve.wait_ge(s_setp, 1)
            for i in range(3):
                w = min(CH, 9 * P - i * CH)
                link(v.tensor_copy(turned[:, i * CH:i * CH + w], bank[i][:, 0:w]))
            link(v.tensor_copy(mats["Wa"][:, :], turned[:, 0:P]))
            link(v.tensor_copy(mats["Wx"][:, :], turned[:, P:2 * P]))
            v.tensor_copy(tcol[:, 0:1], tcol[:, 1:2]).then_inc(s_set, 1)
            dve.wait_ge(s_setp, 2)
            b3 = bank[3]
            link(v.tensor_tensor(mats["Wz"][:, :], b3[:, 0:P], mats["W1a"][:, :], ALU.add))
            link(v.tensor_tensor(c["bz"][:, :], b3[:, P:P + 1], c["b1"][:, :], ALU.add))
            for k in (1, 2):
                link(v.tensor_copy(dst8[k][:, :], b3[:, P + 8 * k:P + 8 * k + 8]))
            for h in range(HEADS):
                link(v.tensor_copy(src8[3][:, h:h + 1], b3[:, P + 32 + 2 * h:P + 33 + 2 * h]))
                link(v.tensor_copy(dst8[3][:, h:h + 1], b3[:, P + 33 + 2 * h:P + 34 + 2 * h]))
            link(v.tensor_tensor(dst8[3][:, HEADS:], src8[3][:, 0:HEADS], dst8[3][:, 0:HEADS], ALU.add))
            dve.wait_ge(s_setp, 3)
            link(v.tensor_copy(frow[:, :], bank[4][0:1, 0:2 * NT]))
            with dve.Fori(0, 5) as it:
                for l in range(2):
                    dve.wait_ge(s_mk[l], it * 16 + 16)
                    v.tensor_tensor(same[:, bass.ds(it * (2 * MB) + l * MB, MB)], mbuf[l][:, 1:MB + 1],
                                    mbuf[l][:, 0:MB], ALU.is_equal).then_inc(s_mask, 1)

        def setup_tensor(pe):
            t = nc.tensor
            pe.wait_ge(s_seta, 2)
            pe.wait_ge(s_w, 16 * len(loads))
            sources = [tmp_a, tmp_x, mats["Wd0"][:, :], mats["V1"][:, :], mats["V2"][:, :]] + \
                      [V3[:, h * P:(h + 1) * P] for h in range(HEADS)]
            for i, m in enumerate(sources):
                last = t.transpose(bank[i // 4][:, (i % 4) * P:(i % 4 + 1) * P], m, ident[:, :])
            last.then_inc(s_setp, 1)
            pe.wait_ge(s_set, 2)
            b3 = bank[3]

            def T_(i):
                return turned[:, i * P:(i + 1) * P]

            t.matmul(b3[:, 0:P], T_(2), mats["W1b"][:, :], start=True, stop=True)
            t.matmul(b3[:, P:P + 1], mats["W1b"][:, :], c["bm"][:, :], start=True, stop=True)
            for k in (1, 2):
                t.matmul(b3[:, P + 8 * k:P + 8 * k + 8], T_(2 + k), comb[k][:, :], start=True, stop=True)
            for h in range(HEADS):
                last = t.matmul(b3[:, P + 32 + 2 * h:P + 34 + 2 * h], T_(5 + h), asd[3][:, h::HEADS], start=True, stop=True)
            last.then_inc(s_setp, 1)
            pe.wait_ge(s_set, 1)
            for i, (m, col) in enumerate((("pre", P - 1), ("pre", 2 * P - 1), ("suf", 0), ("suf", P))):
                last = t.transpose(bank[4][0:1, i * RP:(i + 1) * RP], R[m][:, col:col + 1], ident[0:RP, 0:RP])
            last.then_inc(s_setp, 1)

        def setup_scalar(act):
            pass

        def setup_pool(pool):
            g = nc.gpsimd
            g.memset(ident[:, :], 0.0).then_inc(s_seta, 1)
            pool.wait_ge(s_seta, 1)
            g.affine_select(out=ident[:, :], in_=ident[:, :], compare_op=ALU.not_equal, fill=1.0, base=0,
                            pattern=[[-1, P]], channel_multiplier=1).then_inc(s_seta, 1)
            g.iota(slot_row, pattern=[[P, NT]], base=NP, channel_multiplier=1).then_inc(s_seta, 1)
            g.iota(node_iota, pattern=[[1, NP // P]], base=0, channel_multiplier=NP // P).then_inc(s_seta, 1)
            pool.wait_ge(s_seta, 4)
            pool.dma_start(node_row.rearrange("(p j) o -> p (j o)", p=P), node_iota).then_inc(s_sc, 16)
            pool.wait_ge(s_sc, 16)
            pool.wait_ge(s_map, 1)

        def map_pool(pool):
            g = nc.gpsimd
            with pool.Fori(0, EIT) as it:
                for l in range(EL):
                    g.tensor_copy(idx[l][:, :], last_row[:, bass.ds(it * (EL * TILES) + l * TILES, TILES)])
                    g.tensor_copy(idx2[l][:, :], slot_row[:, bass.ds(it * (EL * TILES) + l * TILES, TILES)])\
                     .then_inc(s_pool, 1)
                pool.wait_ge(s_pool, it * EL + EL)
                settle(pool, s_dsc)
                for l in range(EL):
                    for j in range(TILES):
                        pool.indirect_dma_start(node_row, bass.IndirectOffsetOnAxis(ap=idx[l][:, j:j + 1], axis=0),
                                                idx2[l][:, j:j + 1], None, bounds_check=NP - 1,
                                                oob_is_err=False).then_inc(s_sc, 16)
                pool.wait_ge(s_sc, it * (16 * EL * TILES) + (16 * EL * TILES + 16))
                settle(pool, s_dsc)
            with pool.Fori(0, EIT) as it:
                for l in range(EL):
                    g.tensor_copy(idx[l][:, :], src_col[:, bass.ds(it * (EL * TILES) + l * TILES, TILES)])\
                     .then_inc(s_pool, 1)
                pool.wait_ge(s_pool, it * EL + (EL * EIT + EL))
                settle(pool, s_dsc)
                for l in range(EL):
                    for j in range(TILES):
                        pool.indirect_dma_start(idx2[l][:, j:j + 1], None, node_row,
                                                bass.IndirectOffsetOnAxis(ap=idx[l][:, j:j + 1], axis=0))\
                            .then_inc(s_sc2, 16)
                pool.wait_ge(s_sc2, it * (16 * EL * TILES) + 16 * EL * TILES)
                settle(pool, s_dsc)
                for l in range(EL):
                    last = g.tensor_copy(gather_row[:, bass.ds(it * (EL * TILES) + l * TILES, TILES)], idx2[l][:, :])
                last.then_inc(s_gr, 1)
                pool.wait_ge(s_gr, it + 1)
                settle(pool, s_dsc)
            for i, (cols, target) in enumerate(((src_col, staged), (dst_col, own[0]))):
                with pool.Fori(0, EIT) as it:
                    for l in range(EL):
                        g.tensor_copy(idx[l][:, :], cols[:, bass.ds(it * (EL * TILES) + l * TILES, TILES)])\
                         .then_inc(s_pool, 1)
                    pool.wait_ge(s_pool, it * EL + ((2 + i) * EL * EIT + EL))
                    settle(pool, s_dsc)
                    for l in range(EL):
                        for j in range(TILES):
                            pool.indirect_dma_start(rows(B[l])[:, j, :], None, a["x"],
                                                    bass.IndirectOffsetOnAxis(ap=idx[l][:, j:j + 1], axis=0))\
                                .then_inc(s_zg, 16)
                    pool.wait_ge(s_zg, it * (16 * EL * TILES) + 16 * EL * TILES * (1 + i * EIT))
                    settle(pool, s_dsc)
                    for l in range(EL):
                        pool.dma_start(slot_rows(target, at(it, l)), rows(B[l])).then_inc(s_zs, 16)
                    pool.wait_ge(s_zs, it * (16 * EL) + 16 * EL * (1 + i * EIT))
                    settle(pool, s_dsc)

        def chunk_rows(tensor, it, lane):
            return tensor[bass.ds(it * (DL * CH) + lane * CH, CH), :].rearrange("(p j) f -> p (j f)", j=TILES)

        def norm_or_stage(eng, ready, it, l):
            if isinstance(ready, int):
                eng.wait_ge(LND["out"].sem, LND["out"].done(it * (4 * DL) + (ready * DL + l)))
            else:
                eng.wait_ge(ready.sem, ready.done(it, l))

        def dense_sync(sp):
            def load(it):
                for l in range(DL):
                    sp.dma_start(d["z"][l], chunk_rows(a["x"], it, l)).then_inc(s_z[l], 16)

            def body(it, more):
                if more:
                    for l in range(DL):
                        sp.wait_ge(D["zb"].sem, D["zb"].done(it, l))
                        settle(sp, s_sync)
                        sp.wait_ge(D["t0"].sem, D["t0"].done(it, l))
                        settle(sp, s_sync)
                        sp.dma_start(d["z"][l], chunk_rows(a["x"], it + 1, l)).then_inc(s_z[l], 16)
                for buf, ready, target in (("xs0", D["xs0"], table[1]), ("xs1", D["xs1"], table[2]),
                                           ("xs2", D["xs2"], table[3]), ("x4", 1, table[4]),
                                           ("p5", D["p5"], table[5]), ("p6", D["p6"], table[6]),
                                           ("x7", D["x7"], table[7]), ("xo", 3, out)):
                    for l in range(DL):
                        norm_or_stage(sp, ready, it, l)
                        settle(sp, s_sync)
                        sp.dma_start(chunk_rows(target, it, l), d[buf][l]).then_inc(s_zo[l], 16)
                for l in range(DL):
                    sp.wait_ge(s_zo[l], it * (16 * 8) + 16 * 8)
                    sp.sem_inc(D["stored"].sem, 1)

            load(0)
            with sp.Fori(0, DIT - 1) as it:
                body(it, True)
            body(DIT - 1, False)

        def dense_tensor(pe):
            def t(it, buf, ready, signal, first=False):
                for l in range(DL):
                    n = it * DL + l
                    if first:
                        pe.wait_ge(s_z[l], it * 16 + 16)
                        pe.wait_ge(D["y3"].sem, D["y3"].done_before(it, l))
                    else:
                        norm_or_stage(pe, ready, it, l)
                    transpose4(d[buf][l], bank[l]).then_inc(D[signal].sem, 1)

            def r(it, buf, ready, mat, signal):
                for l in range(DL):
                    pe.wait_ge(ready.sem, ready.done(it, l))
                    rows4(d[buf][l], mats[mat], bank[l]).then_inc(D[signal].sem, 1)

            with pe.Fori(0, DIT) as it:
                t(it, "z", None, "t0", first=True)
                for l in range(DL):
                    pe.wait_ge(D["f0"].sem, D["f0"].done(it, l))
                    nc.tensor.matmul(bank[l][:, :], mats["W1a"][:, :], d["f0"][l], start=True, stop=True)\
                      .then_inc(D["m0"].sem, 1)
                r(it, "f1", D["f1"], "W2", "r0")
                t(it, "x1", 0, "t1")
                r(it, "f0", D["f0b"], "gS0", "r1")
                t(it, "xs0", D["xs0"], "t2")
                r(it, "f1", D["f1b"], "gS1", "r2")
                t(it, "xs1", D["xs1"], "t3")
                r(it, "f0", D["f0c"], "gS2", "r3")
                t(it, "x4", 1, "t4")
                r(it, "f1", D["f1c"], "Wx", "r4")
                t(it, "x5", 2, "t5")
                r(it, "f0", D["f0d"], "V1", "r5")
                t(it, "p5", D["p5"], "t6")
                r(it, "f1", D["f1d"], "V2", "r6")
                t(it, "p6", D["p6"], "t7")
                t(it, "f0", D["f0e"], "t8")
                r(it, "f0", D["x7"], "V3m", "r7")

        def dense_scalar(act):
            def f(it, ready, buf, signal, func=ACT.Copy, bias=None, stored=False):
                for l in range(DL):
                    act.wait_ge(ready.sem, ready.done(it, l))
                    if stored:
                        act.wait_ge(D["stored"].sem, D["stored"].done_before(it, l))
                    kw = {} if bias is None else {"bias": bias[:, :]}
                    nc.scalar.activation(d[buf][l], bank[l][:, :], func, **kw).then_inc(D[signal].sem, 1)

            with act.Fori(0, DIT) as it:
                f(it, D["t0"], "f0", "f0")
                f(it, D["m0"], "f1", "f1", ACT.Relu, c["b1"])
                norm_scalar(act, LND, DL, it * (4 * DL))
                f(it, D["t1"], "f0", "f0b")
                f(it, D["r1"], "xs0", "xs0", stored=True)
                f(it, D["t2"], "f1", "f1b", ACT.Relu, c["gb0"])
                f(it, D["r2"], "xs1", "xs1")
                f(it, D["t3"], "f0", "f0c", ACT.Relu, c["gb1"])
                f(it, D["r3"], "xs2", "xs2")
                norm_scalar(act, LND, DL, it * (4 * DL) + 1 * DL)
                f(it, D["t4"], "f1", "f1c")
                norm_scalar(act, LND, DL, it * (4 * DL) + 2 * DL)
                f(it, D["t5"], "f0", "f0d")
                f(it, D["r5"], "p5", "p5")
                f(it, D["t6"], "f1", "f1d", ACT.Relu, c["vb1"])
                f(it, D["r6"], "p6", "p6")
                f(it, D["t7"], "f0", "f0e", ACT.Relu, c["vb2"])
                f(it, D["t8"], "x7", "x7")
                norm_scalar(act, LND, DL, it * (4 * DL) + 3 * DL)

        def norm_scalar(act, LN, lanes, n0):
            for l in range(lanes):
                act.wait_ge(LN["var"].sem, LN["var"].done(n0 + l))
                nc.scalar.activation(sd[:, l, :], mv[:, l, :, 1], ACT.Sqrt, bias=eps[:, :])\
                  .then_inc(LN["sd"].sem, 1)

        def norm_vector(dve, LN, lanes, n0, ready, ready_sem, src, dst):
            v = nc.vector
            for l in range(lanes):
                dve.wait_ge(ready_sem, ready(l))
                for j in range(TILES):
                    last = v.bn_stats(st[:, l, j, :], src[l][:, j * P:(j + 1) * P])
                last.then_inc(LN["st"].sem, 1)
            for l in range(lanes):
                dve.wait_ge(LN["st"].sem, LN["st"].done(n0 + l))
                settle(dve, s_settle)
                for j in range(TILES):
                    last = v.bn_aggr(mv[:, l, j, :], st[:, l, j, :])
                last.then_inc(LN["var"].sem, 1)
            for l in range(lanes):
                dve.wait_ge(LN["sd"].sem, LN["sd"].done(n0 + l))
                v.reciprocal(rs[:, l, :], sd[:, l, :]).then_inc(LN["rs"].sem, 1)
            for l in range(lanes):
                dve.wait_ge(LN["rs"].sem, LN["rs"].done(n0 + l))
                for j in range(TILES):
                    last = v.tensor_scalar(dst[l][:, j * P:(j + 1) * P], src[l][:, j * P:(j + 1) * P],
                                           mv[:, l, j, 0:1], rs[:, l, j:j + 1], ALU.subtract, ALU.mult)
                last.then_inc(LN["out"].sem, 1)

        def over_rows(vec):
            return vec[:, :].unsqueeze(1).to_broadcast([P, TILES, P])

        def dense_vector(dve):
            v = nc.vector

            def plus(it, out_, in0, vec, ready, signal):
                for l in range(DL):
                    if ready is None:
                        dve.wait_ge(s_z[l], it * 16 + 16)
                    else:
                        norm_or_stage(dve, ready, it, l)
                    v.tensor_tensor(rows(d[out_][l]), rows(d[in0][l]), over_rows(bc[vec]), ALU.add)\
                     .then_inc(D[signal].sem, 1)

            def residual(it, ready, other, also, signal):
                for l in range(DL):
                    dve.wait_ge(ready.sem, ready.done(it, l))
                    dve.wait_ge(also.sem, also.done(it, l))
                    v.tensor_tensor(d["y"][l], bank[l][:, :], d[other][l], ALU.add).then_inc(D[signal].sem, 1)

            with dve.Fori(0, DIT) as it:
                plus(it, "zb", "z", "b2", None, "zb")
                residual(it, D["r0"], "zb", D["zb"], "y0")
                norm_vector(dve, LND, DL, it * (4 * DL) + 0 * DL, lambda l: D["y0"].done(it, l), D["y0"].sem, d["y"], d["x1"])
                plus(it, "y", "xs2", "gb2", D["xs2"], "ya")
                for l in range(DL):
                    dve.wait_ge(D["ya"].sem, D["ya"].done(it, l))
                    v.scalar_tensor_tensor(d["y"][l], d["y"][l], 0.0, d["x1"][l], ALU.max, ALU.add)\
                     .then_inc(D["y1"].sem, 1)
                for l in range(DL):
                    dve.wait_ge(D["stored"].sem, D["stored"].done_before(it, l))
                    settle(dve, s_settle)
                norm_vector(dve, LND, DL, it * (4 * DL) + 1 * DL, lambda l: D["y1"].done(it, l), D["y1"].sem, d["y"], d["x4"])
                plus(it, "xb", "x4", "l2", 1, "xb")
                residual(it, D["r4"], "xb", D["xb"], "y2")
                norm_vector(dve, LND, DL, it * (4 * DL) + 2 * DL, lambda l: D["y2"].done(it, l), D["y2"].sem, d["y"], d["x5"])
                plus(it, "xb", "x5", "b3", 2, "xb5")
                residual(it, D["r7"], "xb", D["xb5"], "y3")
                norm_vector(dve, LND, DL, it * (4 * DL) + 3 * DL, lambda l: D["y3"].done(it, l), D["y3"].sem, d["y"], d["xo"])

        def gather4(pool, stage, cols, use, it, i2, par, source, free):
            for l in range(EL):
                n = num(use, it, l)
                for f in free:
                    pool.wait_ge(f.sem, f.done(n - 2 * EL))
                    settle(pool, s_dsc)
                nc.gpsimd.tensor_copy(IDX[par][l][:, :], cols[:, bass.ds(it * (EL * TILES) + l * TILES, TILES)])\
                  .then_inc(stage.sem, 1)
                pool.wait_ge(stage.sem, stage.done(n))
                settle(pool, s_dsc)
                for j in range(TILES):
                    pool.indirect_dma_start(rows(GG[par][l])[:, j, :], None, source,
                                            bass.IndirectOffsetOnAxis(ap=IDX[par][l][:, j:j + 1], axis=0))\
                        .then_inc(s_gather[par][l], 16)

        GG, IDX, s_gather = (G, H), (idx, idx2), (s_ga, s_gb)

        def gathered(eng, phase, k, i2, par, l):
            before = sum(dmas("gathered", *p) for p in FULL_ORDER[:FULL_ORDER.index((phase, k))])
            eng.wait_ge(s_gather[par][l], i2 * (16 * TILES) + (16 * before * (EIT // 2) + 16 * TILES))

        def wait_chunk(eng, stage, n):
            eng.wait_ge(stage.sem, stage.done(n))

        def spread_mask(e0):
            return same[:, bass.ds(e0 + 1, CH)]

        def put_state(dve, src, it, l, signal):
            e0 = at(it, l)
            nc.vector.scalar_tensor_tensor(state[:, bass.ds(e0, CH)], spread_mask(e0), 0.0, src,
                                           ALU.is_equal, ALU.mult).then_inc(signal.sem, 1)

        TAILS = [dict(bias="b2", res=own[0], base=0, keep=[(own[1], 0)], mat="gS0", to=table[1], relu=None),
                 dict(bias=None, res=own[1], base=0, keep=[(table[4], NP)], mat=None, to=None, relu="gb2"),
                 dict(bias="l2", res=table[4], base=NP, keep=[(own[5], 0)], mat="V1", to=table[5], relu=None),
                 dict(bias="b3", res=own[5], base=0, keep=[], mat=None, to=None, relu=None)]
        FULL_ORDER = [("first", 0), ("weights", 0), ("tail", 0)]
        for k in range(3):
            FULL_ORDER += [("scores2", k), ("weights", 1 + k), ("combine", k), ("spread", k) if k < 2 else ("tail", 1)]
        FULL_ORDER += [("mean", 0), ("tail", 2)]
        for k in range(2):
            FULL_ORDER += [("scores4", k), ("weights", 4 + k), ("combine", 3 + k), ("spread", 2 + k)]
        FULL_ORDER += [("scores4", 2), ("weights", 6), ("heads", 0), ("tail", 3)]

        def dmas(what, phase, k):
            tail_stores = len(TAILS[k]["keep"]) + (TAILS[k]["mat"] is not None) if phase == "tail" else 0
            return {"store": {"scores2": 2, "scores4": 2, "spread": 1, "tail": tail_stores},
                    "load": {"first": 1, "combine": 1, "heads": 1},
                    "load_own": {"first": 1, "tail": 1, "combine": 1, "heads": 1},
                    "gathered": {"scores2": TILES, "mean": TILES, "scores4": TILES}}[what].get(phase, 0)

        def landed(what, phase, k, it):
            before = sum(dmas(what, *p) for p in FULL_ORDER[:FULL_ORDER.index((phase, k))])
            per = dmas(what, phase, k)
            return it * (16 * per) + 16 * (before * EIT + per)

        def first_sync(sp, use):
            with sp.Fori(0, EIT) as it:
                for l in range(EL):
                    n = num(0, it, l)
                    wait_chunk(sp, E0["scan"], n - EL)
                    settle(sp, s_sync)
                    sp.dma_start(rows(G[l]), slot_rows(staged, at(it, l))).then_inc(s_in[l], 16)
                    wait_chunk(sp, E0["hT"], n - EL)
                    settle(sp, s_sync)
                    sp.dma_start(rows(H[l]), slot_rows(own[0], at(it, l))).then_inc(s_in2[l], 16)
                    wait_chunk(sp, E0["m"], n - EL)
                    settle(sp, s_sync)
                    sp.dma_start(ew[:, l * CH:(l + 1) * CH], a["ew"][bass.ds(at(it, l), CH)].unsqueeze(0))\
                      .then_inc(s_ew[l], 16)

        def first_pool(pool, use):
            pass

        def first_tensor(pe, use):
            t = nc.tensor
            with pe.Fori(0, EIT) as it:
                for l in range(EL):
                    pe.wait_ge(s_in[l], landed("load", "first", 0, it))
                    wait_chunk(pe, E0["state"], num(0, it, l) - EL)
                    transpose4(G[l], bank[l]).then_inc(E0["gT"].sem, 1)
                for l in range(EL):
                    pe.wait_ge(s_in2[l], landed("load_own", "first", 0, it))
                    wait_chunk(pe, E0["a"], num(0, it, l))
                    transpose4(H[l], bank[l]).then_inc(E0["hT"].sem, 1)
                for l in range(EL):
                    wait_chunk(pe, E0["s"], num(0, it, l))
                    pe.wait_ge(s_ew[l], it * 16 + 16)
                    t.matmul(bank[l][:, :], mats["Ws0"][:, :], A[l], start=True, stop=False)
                    t.matmul(bank[l][:, :], ww[:, :], ew[:, l * CH:(l + 1) * CH], start=False, stop=True)\
                     .then_inc(E0["m"].sem, 1)
                for l in range(EL):
                    wait_chunk(pe, E0["scan"], num(0, it, l))
                    t.matmul(bank[l][:, :], mats["W1b"][:, :], B[l], start=True, stop=False)
                    t.matmul(bank[l][:, :], mats["Wz"][:, :], state[:, bass.ds(at(it, l), CH)], start=False, stop=True)\
                     .then_inc(E0["h"].sem, 1)
                for l in range(EL):
                    wait_chunk(pe, E0["r"], num(0, it, l))
                    t.matmul(bank[l][:, :], mats["W2"][:, :], A[l], start=True, stop=True).then_inc(E0["o"].sem, 1)

        def first_scalar(act, use):
            with act.Fori(0, EIT) as it:
                for l in range(EL):
                    wait_chunk(act, E0["gT"], num(0, it, l))
                    nc.scalar.activation(A[l], bank[l][:, :], ACT.Copy).then_inc(E0["a"].sem, 1)
                for l in range(EL):
                    wait_chunk(act, E0["hT"], num(0, it, l))
                    nc.scalar.activation(state[:, bass.ds(at(it, l), CH)], bank[l][:, :], ACT.Copy)\
                      .then_inc(E0["s"].sem, 1)
                for l in range(EL):
                    wait_chunk(act, E0["h"], num(0, it, l))
                    nc.scalar.activation(A[l], bank[l][:, :], ACT.Relu, bias=c["bz"][:, :]).then_inc(E0["r"].sem, 1)

        def first_vector(dve, use):
            v = nc.vector
            v.memset(B[EL - 1][:, CH - 1:CH], NEG).then_inc(s_cz, 1)
            dve.wait_ge(s_cz, 1)
            with dve.Fori(0, EIT) as it:
                for l in range(EL):
                    wait_chunk(dve, E0["gT"], num(0, it, l))
                    v.tensor_scalar(G[l], same[:, bass.ds(at(it, l), CH)], -1.0, -NEG, ALU.add, ALU.mult)\
                     .then_inc(E0["neg"].sem, 1)
                for l in range(EL):
                    n = num(0, it, l)
                    wait_chunk(dve, E0["neg"], n)
                    wait_chunk(dve, E0["m"], n)
                    wait_chunk(dve, E0["scan"], n - 1)
                    v.tensor_tensor_scan(B[l], G[l], bank[l][:, :], B[(l - 1) % EL][:, CH - 1:CH], ALU.add, ALU.max)\
                     .then_inc(E0["scan"].sem, 1)
                for l in range(EL):
                    wait_chunk(dve, E0["o"], num(0, it, l))
                    put_state(dve, bank[l][:, :], it, l, E0["state"])

        MATS = [0, 1, 1, 2, 2]
        BIAS = [0, 1, 1, 2, 3]

        PIECE = EL * CH

        def spread_runs(stage, use):
            for i in reversed(range(EIT)):
                mask, piece = same[:, i * PIECE + 1:(i + 1) * PIECE + 1], state[:, i * PIECE:(i + 1) * PIECE]
                nc.vector.wait_ge(stage.sem, stage.done((use * EIT + EIT - 1 - i) * EL - 1))
                carry_ = 0.0 if i == EIT - 1 else carry[:, 0:1]
                nc.vector.tensor_tensor_scan(piece[:, ::-1], mask[:, ::-1], piece[:, ::-1], carry_, ALU.mult, ALU.add)                  .then_inc(s_cz, 1)
                cz[0] += 1
                nc.vector.wait_ge(s_cz, cz[0])
                nc.vector.tensor_copy(carry[:, 0:1], piece[:, 0:1]).then_inc(stage.sem, EL)

        def tail_sync(sp, k):
            tl = TAILS[k]
            with sp.Fori(0, EIT) as it:
                for l in range(EL):
                    n = num(k, it, l)
                    wait_chunk(sp, TL["stored"], n - EL)
                    settle(sp, s_sync)
                    if k < 3:
                        wait_chunk(sp, TL["xt"], n - EL)
                        settle(sp, s_sync)
                    sp.dma_start(rows(H[l]), slot_rows(tl["res"], at_back(it, l), tl["base"])).then_inc(s_in2[l], 16)
                if tl["keep"]:
                    for l in range(EL):
                        wait_chunk(sp, LNS["out"], num(k, it, l))
                        settle(sp, s_sync)
                        (target, base), = tl["keep"]
                        sp.dma_start(slot_rows(target, at_back(it, l), base), rows(H[l])).then_inc(s_st[l], 16)
                if tl["mat"]:
                    for l in range(EL):
                        wait_chunk(sp, TL["g"], num(MATS[k], it, l))
                        settle(sp, s_sync)
                        sp.dma_start(slot_rows(tl["to"], at_back(it, l), NP), rows(G[l])).then_inc(s_st[l], 16)
                for l in range(EL):
                    if tl["keep"]:
                        sp.wait_ge(s_st[l], landed("store", "tail", k, it))
                        settle(sp, s_sync)
                    else:
                        wait_chunk(sp, TL["cp"], num(k, it, l))
                    sp.sem_inc(TL["stored"].sem, 1)

        def tail_pool(pool, k):
            tl = TAILS[k]
            with pool.Fori(0, EIT) as it:
                if tl["bias"]:
                    for l in range(EL):
                        pool.wait_ge(s_in2[l], landed("load_own", "tail", k, it))
                        settle(pool, s_dsc)
                        nc.gpsimd.tensor_tensor(rows(H[l]), rows(H[l]), over_rows(bc[tl["bias"]]), ALU.add)\
                          .then_inc(TL["b"].sem, 1)
                if k < 3:
                    for l in range(EL):
                        wait_chunk(pool, TL["x"], num(k, it, l))
                        settle(pool, s_dsc)
                        nc.gpsimd.tensor_copy(state[:, bass.ds(at_back(it, l), CH)], B[l]).then_inc(TL["cp"].sem, 1)
                else:
                    for l in range(EL):
                        e0 = (ECH - 1) * TILES - l * TILES - it * (EL * TILES)
                        nc.gpsimd.tensor_copy(idx[l][:, :], last_row[:, bass.ds(e0, TILES)]).then_inc(TL["idx"].sem, 1)
                        pool.wait_ge(TL["idx"].sem, TL["idx"].done(it * EL + l))
                        settle(pool, s_dsc)
                        wait_chunk(pool, LNS["out"], num(k, it, l))
                        settle(pool, s_dsc)
                        for j in range(TILES):
                            pool.indirect_dma_start(out, bass.IndirectOffsetOnAxis(ap=idx[l][:, j:j + 1], axis=0),
                                                    rows(H[l])[:, j, :], None, bounds_check=NP - 1,
                                                    oob_is_err=False).then_inc(s_out[l], 16)
                    for l in range(EL):
                        pool.wait_ge(s_out[l], it * (16 * TILES) + 16 * TILES)
                        settle(pool, s_dsc)
                        pool.sem_inc(TL["cp"].sem, 1)

        def tail_scalar(act, k):
            tl = TAILS[k]
            with act.Fori(0, EIT) as it:
                for l in range(EL):
                    n = num(k, it, l)
                    wait_chunk(act, TL["s"], n)
                    if k < 3:
                        wait_chunk(act, TL["cp"], n - EL)
                    else:
                        wait_chunk(act, TL["t"], n - EL)
                    if tl["relu"]:
                        ins = nc.scalar.activation(B[l], state[:, bass.ds(at_back(it, l), CH)], ACT.Relu, bias=c[tl["relu"]][:, :])
                    else:
                        ins = nc.scalar.activation(B[l], state[:, bass.ds(at_back(it, l), CH)], ACT.Copy)
                    ins.then_inc(TL["a"].sem, 1)
                norm_scalar(act, LNS, EL, it * EL + k * ECH)
                for l in range(EL if k < 3 else 0):
                    wait_chunk(act, TL["xt"], num(k, it, l))
                    nc.scalar.activation(B[l], bank[l][:, :], ACT.Copy).then_inc(TL["x"].sem, 1)
                if tl["mat"]:
                    for l in range(EL):
                        wait_chunk(act, TL["r"], num(MATS[k], it, l))
                        nc.scalar.activation(G[l], bank[l][:, :], ACT.Copy).then_inc(TL["g"].sem, 1)

        def tail_vector(dve, k):
            tl = TAILS[k]
            v = nc.vector
            spread_runs(TL["s"], k)
            with dve.Fori(0, EIT) as it:
                for l in range(EL):
                    n = num(k, it, l)
                    if tl["bias"]:
                        wait_chunk(dve, TL["b"], num(BIAS[k], it, l))
                    else:
                        dve.wait_ge(s_in2[l], landed("load_own", "tail", k, it))
                    wait_chunk(dve, TL["stored"], n - EL)
                    wait_chunk(dve, TL["t"], n)
                    v.tensor_tensor(G[l], bank[l][:, :], H[l], ALU.add).then_inc(TL["y"].sem, 1)
                norm_vector(dve, LNS, EL, it * EL + k * ECH, lambda l: TL["y"].done(num(k, it, l)), TL["y"].sem, G, H)

        def tail_tensor(pe, k):
            tl = TAILS[k]
            with pe.Fori(0, EIT) as it:
                for l in range(EL):
                    n = num(k, it, l)
                    wait_chunk(pe, TL["a"], n)
                    if tl["mat"]:
                        wait_chunk(pe, TL["g"], num(MATS[k], it, l) - EL)
                    wait_chunk(pe, TL["x"] if k < 3 else TL["y"], n - EL)
                    transpose4(B[l], bank[l]).then_inc(TL["t"].sem, 1)
                for l in range(EL if k < 3 else 0):
                    wait_chunk(pe, LNS["out"], num(k, it, l))
                    transpose4(H[l], bank[l]).then_inc(TL["xt"].sem, 1)
                if tl["mat"]:
                    for l in range(EL):
                        wait_chunk(pe, TL["x"], num(k, it, l))
                        rows4(B[l], mats[tl["mat"]], bank[l]).then_inc(TL["r"].sem, 1)

        SPREADS = [dict(bias="gb0", mat="gS1", to=table[2]), dict(bias="gb1", mat="gS2", to=table[3]),
                   dict(bias="vb1", mat="V2", to=table[6]), dict(bias="vb2", mat=None, to=table[7])]

        def spread_sync(sp, k):
            with sp.Fori(0, EIT) as it:
                for l in range(EL):
                    wait_chunk(sp, SP_["g"], num(k, it, l))
                    settle(sp, s_sync)
                    sp.dma_start(slot_rows(SPREADS[k]["to"], at_back(it, l), NP), rows(G[l])).then_inc(s_st[l], 16)
                for l in range(EL):
                    sp.wait_ge(s_st[l], landed("store", "spread", k, it))
                    sp.sem_inc(SP_["stored"].sem, 1)

        def spread_pool(pool, k):
            with pool.Fori(0, EIT) as it:
                for l in range(EL):
                    wait_chunk(pool, SP_["a"], num(k, it, l))
                    settle(pool, s_dsc)
                    nc.gpsimd.tensor_copy(state[:, bass.ds(at_back(it, l), CH)], B[l]).then_inc(SP_["cp"].sem, 1)

        def spread_vector(dve, k):
            spread_runs(SP_["s"], k)

        def spread_scalar(act, k):
            with act.Fori(0, EIT) as it:
                for l in range(EL):
                    n = num(k, it, l)
                    wait_chunk(act, SP_["s"], n)
                    wait_chunk(act, SP_["cp"], n - EL)
                    wait_chunk(act, SP_["r"], n - EL)
                    nc.scalar.activation(B[l], state[:, bass.ds(at_back(it, l), CH)], ACT.Relu, bias=c[SPREADS[k]["bias"]][:, :])\
                      .then_inc(SP_["a"].sem, 1)
                for l in range(EL):
                    n = num(k, it, l)
                    wait_chunk(act, SP_["r"], n)
                    wait_chunk(act, SP_["stored"], n - EL)
                    nc.scalar.activation(G[l], bank[l][:, :], ACT.Copy).then_inc(SP_["g"].sem, 1)

        def spread_tensor(pe, k):
            mat = SPREADS[k]["mat"]
            with pe.Fori(0, EIT) as it:
                for l in range(EL):
                    n = num(k, it, l)
                    wait_chunk(pe, SP_["a"], n)
                    wait_chunk(pe, SP_["g"], n - EL)
                    ins = rows4(B[l], mats[mat], bank[l]) if mat else transpose4(B[l], bank[l])
                    ins.then_inc(SP_["r"].sem, 1)

        def scores2_sync(sp, k):
            with sp.Fori(0, EIT // 2) as i2:
                for par in range(2):
                    it = i2 * 2 + par
                    for l in range(EL):
                        gathered(sp, "scores2", k, i2, par, l)
                        settle(sp, s_sync)
                        sp.dma_start(slot_rows(staged, at(it, l)), rows(GG[par][l])).then_inc(s_st[l], 16)
                    for l in range(EL):
                        wait_chunk(sp, GA["row"], num(k, it, l))
                        settle(sp, s_sync)
                        sp.dma_start(scores[0:1, bass.ds(at(it, l), CH)], score_rows[l][0:1, :]).then_inc(s_st[l], 16)
                    for l in range(EL):
                        sp.wait_ge(s_st[l], landed("store", "scores2", k, it))
                        sp.sem_inc(GA["stored"].sem, 1)

        def scores2_pool(pool, k):
            with pool.Fori(0, EIT // 2) as i2:
                for par in range(2):
                    it = i2 * 2 + par
                    gather4(pool, GA["idx"], gather_row, k, it, i2, par, table[1 + k], [GA["pre"], GA["stored"]])

        def scores2_tensor(pe, k):
            t = nc.tensor
            with pe.Fori(0, EIT // 2) as i2:
                for par in range(2):
                    it = i2 * 2 + par
                    for l in range(EL):
                        gathered(pe, "scores2", k, i2, par, l)
                        wait_chunk(pe, GA["row"], num(k, it, l) - EL)
                        t.matmul(bank[l][:, :], mats[f"gD{k}"][:, :], state[:, bass.ds(at(it, l), CH)], start=True, stop=False)
                        for j in range(TILES):
                            last = t.matmul(bank[l][:, j * P:(j + 1) * P], GG[par][l][:, j * P:(j + 1) * P], ident[:, :],
                                            start=False, stop=(j == TILES - 1), is_transpose=TRANSPOSE_ADDS)
                        last.then_inc(GA["pre"].sem, 1)
                    for l in range(EL):
                        wait_chunk(pe, GA["a"], num(k, it, l))
                        t.matmul(bank[l][:, :], mats[f"gB{k}"][:, :], state[:, bass.ds(at(it, l), CH)], start=True, stop=True)\
                         .then_inc(GA["self"].sem, 1)
                    for l in range(EL):
                        wait_chunk(pe, GA["la"], num(k, it, l))
                        wait_chunk(pe, GA["lb"], num(k, it, l))
                        t.matmul(bank[l][0:1, :], c[f"att{k}"][:, :], A[l], start=True, stop=False)
                        t.matmul(bank[l][0:1, :], c[f"natt{k}"][:, :], B[l], start=False, stop=True).then_inc(GA["e"].sem, 1)

        def scores2_scalar(act, k):
            with act.Fori(0, EIT // 2) as i2:
                for par in range(2):
                    it = i2 * 2 + par
                    for l in range(EL):
                        wait_chunk(act, GA["pre"], num(k, it, l))
                        nc.scalar.activation(A[l], bank[l][:, :], ACT.Copy).then_inc(GA["a"].sem, 1)
                    for l in range(EL):
                        wait_chunk(act, GA["self"], num(k, it, l))
                        nc.scalar.activation(B[l], bank[l][:, :], ACT.Copy).then_inc(GA["b"].sem, 1)
                    for l in range(EL):
                        wait_chunk(act, GA["stored"], num(k, it, l) - EL)
                        wait_chunk(act, GA["e"], num(k, it, l))
                        nc.scalar.activation(score_rows[l][0:1, :], bank[l][0:1, :], ACT.Copy).then_inc(GA["row"].sem, 1)

        def scores2_vector(dve, k):
            with dve.Fori(0, EIT) as it:
                for ready, buf, signal in (("a", A, "la"), ("b", B, "lb")):
                    for l in range(EL):
                        wait_chunk(dve, GA[ready], num(k, it, l))
                        nc.vector.scalar_tensor_tensor(buf[l], buf[l], SLOPE, buf[l], ALU.mult, ALU.max)\
                          .then_inc(GA[signal].sem, 1)

        def scores4_sync(sp, k):
            with sp.Fori(0, EIT // 2) as i2:
                for par in range(2):
                    it = i2 * 2 + par
                    for l in range(EL):
                        gathered(sp, "scores4", k, i2, par, l)
                        settle(sp, s_sync)
                        sp.dma_start(slot_rows(staged, at(it, l)), rows(GG[par][l])).then_inc(s_st[l], 16)
                    for l in range(EL):
                        wait_chunk(sp, LA["row"], num(k, it, l))
                        settle(sp, s_sync)
                        sp.dma_start(scores[:, bass.ds(at(it, l), CH)], score_rows[l]).then_inc(s_st[l], 16)
                    for l in range(EL):
                        sp.wait_ge(s_st[l], landed("store", "scores4", k, it))
                        sp.sem_inc(LA["stored"].sem, 1)

        def scores4_pool(pool, k):
            with pool.Fori(0, EIT // 2) as i2:
                for par in range(2):
                    it = i2 * 2 + par
                    gather4(pool, LA["idx"], gather_row, k, it, i2, par, table[5 + k], [LA["gT"], LA["stored"]])

        def scores4_tensor(pe, k):
            t = nc.tensor
            with pe.Fori(0, EIT // 2) as i2:
                for par in range(2):
                    it = i2 * 2 + par
                    for l in range(EL):
                        gathered(pe, "scores4", k, i2, par, l)
                        wait_chunk(pe, LA["row"], num(k, it, l) - EL)
                        transpose4(GG[par][l], bank[l]).then_inc(LA["gT"].sem, 1)
                    for l in range(EL):
                        wait_chunk(pe, LA["a"], num(k, it, l))
                        t.matmul(bank[l][0:2 * HEADS, :], src8[k + 1][:, :], A[l], start=True, stop=False)
                        t.matmul(bank[l][0:2 * HEADS, :], dst8[k + 1][:, :], state[:, bass.ds(at(it, l), CH)],
                                 start=False, stop=True).then_inc(LA["e"].sem, 1)

        def scores4_scalar(act, k):
            with act.Fori(0, EIT // 2) as i2:
                for par in range(2):
                    it = i2 * 2 + par
                    for l in range(EL):
                        wait_chunk(act, LA["gT"], num(k, it, l))
                        nc.scalar.activation(A[l], bank[l][:, :], ACT.Copy).then_inc(LA["a"].sem, 1)
                    for l in range(EL):
                        wait_chunk(act, LA["stored"], num(k, it, l) - EL)
                        wait_chunk(act, LA["e"], num(k, it, l))
                        nc.scalar.activation(score_rows[l], bank[l][0:2 * HEADS, :], ACT.Copy)\
                          .then_inc(LA["row"].sem, 1)

        def scores4_vector(dve, k):
            pass

        MEAN, GAT2, GAT = "mean", "gat2", "gat"
        CALLS = [(MEAN, 0, 0)] + [(GAT2, k, 0) for k in range(3)] + [(GAT, k, h) for k in range(3) for h in range(HEADS)]
        TOP = "mf mb mef meb mcar m1 m2 m3 m4 m5 dm".split()
        SUM = "sf sb sef seb scar s1 s2 s3 s4 s5 s6".split()
        VSTEPS = {MEAN: ["w"] + SUM + ["mx", "rec", "alc"],
                  GAT2: TOP + SUM + ["s7", "rec", "al", "as1", "as2", "alc", "asc"],
                  GAT: ["le", "ls", "d"] + TOP + SUM + ["s7", "rec", "al", "as1", "as2", "alc", "asc"]}
        TSTEPS = {MEAN: ["srow", "scol", "tr"]}
        TSTEPS[GAT2] = TSTEPS[GAT] = ["mrow", "mcol", "srow", "scol", "tr"]

        def step(table_, call, name):
            return sum(len(table_[kd]) for kd, _, _ in CALLS[:call]) + table_[CALLS[call][0]].index(name) + 1

        def loads_before(call):
            return 16 * sum({MEAN: 0, GAT2: 1, GAT: 2}[kd] for kd, _, _ in CALLS[:call + 1])

        def calls_of(phase_use):
            return {0: [0], 1: [1], 2: [2], 3: [3], 4: [4, 5, 6, 7], 5: [8, 9, 10, 11], 6: [12, 13, 14, 15]}[phase_use]

        def weights_sync(sp, u):
            for call in calls_of(u):
                kind, k, h = CALLS[call]
                if call != calls_of(u)[0]:
                    sp.wait_ge(s_vs, step(VSTEPS, call - 1, "d"))
                if kind != MEAN:
                    sp.dma_start(compact_sb(T["e"]), compact(scores[h, :])).then_inc(s_ds, 16)
                if kind == GAT:
                    sp.dma_start(compact_sb(T["s"]), compact(scores[HEADS + h, :])).then_inc(s_ds, 16)

        def weights_pool(pool, u):
            pass

        def weights_scalar(act, u):
            for call in calls_of(u):
                if CALLS[call][0] == MEAN:
                    continue
                act.wait_ge(s_vs, step(VSTEPS, call, "dm"))
                nc.scalar.activation(T["w"], T["dm"], ACT.Exp)
                nc.scalar.activation(T["c"], T["m"], ACT.Exp, scale=-1.0).then_inc(s_as, 1)

        def exps_before(call):
            return sum(1 for kd, _, _ in CALLS[:call + 1] if kd != MEAN)

        def weights_tensor(pe, u):
            t = nc.tensor
            for call in calls_of(u):
                kind = CALLS[call][0]
                for q in (("m", "s") if kind != MEAN else ("s",)):
                    pe.wait_ge(s_vs, step(VSTEPS, call, q + "b"))
                    for i, (m, col) in enumerate((("f", P - 1), ("f", 2 * P - 1), ("b", 0), ("b", P))):
                        last = t.transpose(bank[0][0:1, i * RP:(i + 1) * RP], T[m][:, col:col + 1], ident[0:RP, 0:RP])
                    last.then_inc(s_ts, 1)
                    pe.wait_ge(s_vs, step(VSTEPS, call, q + "eb"))
                    for i, off in enumerate((0, RP, NT + 2, NT + 2 + RP)):
                        last = t.matmul(bank[1][0:RP, i:i + 1], erow[0:1, off:off + RP], one[:, :], start=True, stop=True)
                    last.then_inc(s_ts, 1)
                pe.wait_ge(s_vs, step(VSTEPS, call, "as2" if kind != MEAN else "rec"))
                for i, m in enumerate(("t", "u") if kind != MEAN else ("t",)):
                    for g in range(2):
                        last = t.transpose(bank[2][:, i * NT + g * RP:i * NT + (g + 1) * RP], T[m][:, g * P:(g + 1) * P],
                                           ident[0:RP, 0:RP])
                last.then_inc(s_ts, 1)

        def weights_vector(dve, u):
            v = nc.vector
            for call in calls_of(u):
                kind, k, h = CALLS[call]
                names_ = VSTEPS[kind]
                at_ = [0]

                def link(name, ins):
                    assert names_[at_[0]] == name
                    at_[0] += 1
                    ins.then_inc(s_vs, 1)
                    dve.wait_ge(s_vs, step(VSTEPS, call, name))

                def halves(name, out_, flags, col, in1, op, first):
                    for g in range(2):
                        sl = slice(g * P, (g + 1) * P)
                        link(f"{name}{first + g}", v.scalar_tensor_tensor(out_[:, sl], flags[:, sl], ccol[:, col + g:col + g + 1],
                                                                          in1[:, sl], ALU.mult, op))

                def run_totals(q, x, op, total):
                    link(q + "f", v.tensor_tensor_scan(T["f"], R["contz"][:, :], x, 0.0, ALU.mult, op))
                    link(q + "b", v.tensor_tensor_scan(T["b"][:, ::-1], R["contbz"][:, ::-1], x[:, ::-1], 0.0, ALU.mult, op))
                    dve.wait_ge(s_ts, step(TSTEPS, call, q + "row"))
                    link(q + "ef", v.tensor_tensor_scan(erow[:, 1:NT + 1], frow[:, 0:NT], bank[0][0:1, 0:NT], 0.0,
                                                        ALU.mult, op))
                    link(q + "eb", v.tensor_tensor_scan(erow[:, NT + 1:2 * NT + 1][:, ::-1], frow[:, NT:][:, ::-1],
                                                        bank[0][0:1, NT:2 * NT][:, ::-1], 0.0, ALU.mult, op))
                    dve.wait_ge(s_ts, step(TSTEPS, call, q + "col"))
                    link(q + "car", v.tensor_copy(ccol[:, :], bank[1][0:RP, 0:4]))
                    halves(q, total, R["pre"], 0, T["f"], op, 1)
                    halves(q, total, R["suf"], 2, total, op, 3)
                    link(q + "5", v.tensor_tensor(total, total, T["b"], op))

                if kind == MEAN:
                    link("w", v.memset(T["w"], 1.0))
                else:
                    dve.wait_ge(s_ds, loads_before(call))
                    if kind == GAT:
                        link("le", v.scalar_tensor_tensor(T["d"], T["e"], SLOPE, T["e"], ALU.mult, ALU.max))
                        link("ls", v.scalar_tensor_tensor(T["di"], T["s"], SLOPE, T["s"], ALU.mult, ALU.max))
                        link("d", v.tensor_tensor(T["d"], T["d"], T["di"], ALU.subtract))
                        score = T["d"]
                    else:
                        score = T["e"]
                    run_totals("m", score, ALU.max, T["m"])
                    link("dm", v.tensor_tensor(T["dm"], score, T["m"], ALU.subtract))
                    dve.wait_ge(s_as, exps_before(call))
                run_totals("s", T["w"], ALU.add, T["t"])
                link("s6", v.tensor_tensor(T["t"], T["t"], T["w"], ALU.subtract))
                if kind == MEAN:
                    link("mx", v.tensor_scalar(T["t"], T["t"], 1.0, None, ALU.max))
                    link("rec", v.reciprocal(T["t"], T["t"]))
                    dve.wait_ge(s_ts, step(TSTEPS, call, "tr"))
                    link("alc", v.tensor_copy(mean_w[:, :], bank[2][:, 0:NT]))
                    continue
                link("s7", v.scalar_tensor_tensor(T["t"], T["t"], 1e-16 if kind == GAT2 else 0.0, T["c"], ALU.add, ALU.add))
                link("rec", v.reciprocal(T["u"], T["t"]))
                link("al", v.tensor_tensor(T["t"], T["w"], T["u"], ALU.mult))
                link("as1", v.tensor_tensor(T["u"], T["c"], T["u"], ALU.mult))
                link("as2", v.tensor_tensor(T["u"], T["u"], R["start"][:, :], ALU.mult))
                dve.wait_ge(s_ts, step(TSTEPS, call, "tr"))
                al_to, as_to = (alpha[:, 0:NT], aself[:, 0:NT]) if kind == GAT2 else (alpha4[:, :, h], aself4[:, :, h])
                link("alc", v.tensor_copy(al_to, bank[2][:, 0:NT]))
                link("asc", v.tensor_copy(as_to, bank[2][:, NT:2 * NT]))

        def weight_ap(w, it, l, heads):
            if heads == 1:
                return w[:, bass.ds(it * (EL * TILES) + l * TILES, TILES)].unsqueeze(2).to_broadcast([P, TILES, P])
            v4 = w[:, bass.ds(it * (EL * TILES * HEADS) + l * (TILES * HEADS), TILES * HEADS)]
            return v4.unsqueeze(2).to_broadcast([P, TILES * HEADS, P // HEADS])

        def weight_head(w, it, l, h):
            v4 = w[:, bass.ds(it * (EL * TILES * HEADS) + l * (TILES * HEADS), TILES * HEADS)]
            return v4.rearrange("p (j h) -> p j h", h=HEADS)[:, :, h].unsqueeze(2).to_broadcast([P, TILES, P])

        def split(buf, heads):
            return rows(buf) if heads == 1 else buf.rearrange("p (j f) -> p j f", j=TILES * HEADS)

        COMBINES = [(table[1], 1), (table[2], 1), (table[3], 1), (table[5], HEADS), (table[6], HEADS)]

        def combine_sync(sp, k):
            with sp.Fori(0, EIT) as it:
                for l in range(EL):
                    wait_chunk(sp, CA["t"], num(k, it, l) - EL)
                    settle(sp, s_sync)
                    sp.dma_start(rows(G[l]), slot_rows(staged, at(it, l))).then_inc(s_in[l], 16)
                    sp.dma_start(rows(H[l]), slot_rows(COMBINES[k][0], at(it, l), NP)).then_inc(s_in2[l], 16)

        def combine_pool(pool, k):
            heads = COMBINES[k][1]
            with pool.Fori(0, EIT) as it:
                for l in range(EL):
                    pool.wait_ge(s_in2[l], landed("load_own", "combine", k, it))
                    settle(pool, s_dsc)
                    nc.gpsimd.tensor_tensor(split(H[l], heads), split(H[l], heads), weight_ap(aself, it, l, heads), ALU.mult)\
                      .then_inc(CA["h"].sem, 1)

        def combine_vector(dve, k):
            v = nc.vector
            heads = COMBINES[k][1]
            v.memset(A[EL - 1][:, CH - 1:CH], 0.0).then_inc(s_cz, 1)
            cz[0] += 1
            dve.wait_ge(s_cz, cz[0])
            with dve.Fori(0, EIT) as it:
                for l in range(EL):
                    dve.wait_ge(s_in[l], landed("load", "combine", k, it))
                    v.tensor_tensor(split(G[l], heads), split(G[l], heads), weight_ap(alpha, it, l, heads), ALU.mult)\
                     .then_inc(CA["g"].sem, 1)
                for l in range(EL):
                    wait_chunk(dve, CA["g"], num(k, it, l))
                    wait_chunk(dve, CA["h"], num(k, it, l))
                    v.tensor_tensor(G[l], G[l], H[l], ALU.add).then_inc(CA["sum"].sem, 1)
                for l in range(EL):
                    wait_chunk(dve, CA["v"], num(k, it, l) - 1)
                    wait_chunk(dve, CA["t"], num(k, it, l))
                    v.tensor_tensor_scan(A[l], same[:, bass.ds(at(it, l), CH)], bank[l][:, :],
                                         A[(l - 1) % EL][:, CH - 1:CH], ALU.mult, ALU.add).then_inc(CA["v"].sem, 1)
                for l in range(EL):
                    wait_chunk(dve, CA["v"], num(k, it, l))
                    put_state(dve, A[l], it, l, CA["state"])

        def combine_scalar(act, k):
            pass

        def combine_tensor(pe, k):
            with pe.Fori(0, EIT) as it:
                for l in range(EL):
                    wait_chunk(pe, CA["sum"], num(k, it, l))
                    wait_chunk(pe, CA["v"], num(k, it, l) - EL)
                    transpose4(G[l], bank[l]).then_inc(CA["t"].sem, 1)

        def mean_sync(sp, k):
            pass

        def mean_pool(pool, k):
            with pool.Fori(0, EIT // 2) as i2:
                for par in range(2):
                    it = i2 * 2 + par
                    gather4(pool, CM["idx"], gather_row, 0, it, i2, par, table[4], [CM["t"]])

        def mean_vector(dve, k):
            v = nc.vector
            v.memset(A[EL - 1][:, CH - 1:CH], 0.0).then_inc(s_cz, 1)
            cz[0] += 1
            dve.wait_ge(s_cz, cz[0])
            with dve.Fori(0, EIT // 2) as i2:
                for par in range(2):
                    it = i2 * 2 + par
                    for l in range(EL):
                        gathered(dve, "mean", 0, i2, par, l)
                        v.tensor_tensor(rows(GG[par][l]), rows(GG[par][l]), weight_ap(mean_w, it, l, 1), ALU.mult)\
                         .then_inc(CM["g"].sem, 1)
                    for l in range(EL):
                        wait_chunk(dve, CM["v"], num(0, it, l) - 1)
                        wait_chunk(dve, CM["t"], num(0, it, l))
                        v.tensor_tensor_scan(A[l], same[:, bass.ds(at(it, l), CH)], bank[l][:, :],
                                             A[(l - 1) % EL][:, CH - 1:CH], ALU.mult, ALU.add).then_inc(CM["v"].sem, 1)
                    for l in range(EL):
                        wait_chunk(dve, CM["z"], num(0, it, l))
                        put_state(dve, bank[l][:, :], it, l, CM["state"])

        def mean_scalar(act, k):
            pass

        def mean_tensor(pe, k):
            t = nc.tensor
            with pe.Fori(0, EIT // 2) as i2:
                for par in range(2):
                    it = i2 * 2 + par
                    for l in range(EL):
                        wait_chunk(pe, CM["g"], num(0, it, l))
                        wait_chunk(pe, CM["state"], num(0, it, l) - EL)
                        transpose4(GG[par][l], bank[l]).then_inc(CM["t"].sem, 1)
                    for l in range(EL):
                        wait_chunk(pe, CM["v"], num(0, it, l))
                        t.matmul(bank[l][:, :], mats["Wa"][:, :], A[l], start=True, stop=False)
                        t.matmul(bank[l][:, :], mats["Wx"][:, :], state[:, bass.ds(at(it, l), CH)], start=False, stop=True)\
                         .then_inc(CM["z"].sem, 1)

        def head_num(it, h, l):
            return it * (HEADS * EL) + (h * EL + l)

        def heads_sync(sp, k):
            with sp.Fori(0, EIT) as it:
                for l in range(EL):
                    wait_chunk(sp, C3["h"], head_num(it, HEADS - 1, l) - HEADS * EL)
                    settle(sp, s_sync)
                    wait_chunk(sp, C3["g"], head_num(it, HEADS - 1, l) - HEADS * EL)
                    settle(sp, s_sync)
                    sp.dma_start(rows(G[l]), slot_rows(staged, at(it, l))).then_inc(s_in[l], 16)
                    sp.dma_start(rows(H[l]), slot_rows(table[7], at(it, l), NP)).then_inc(s_in2[l], 16)

        def heads_pool(pool, k):
            with pool.Fori(0, EIT) as it:
                for h in range(HEADS):
                    for l in range(EL):
                        if h == 0:
                            pool.wait_ge(s_in2[l], landed("load_own", "heads", 0, it))
                            settle(pool, s_dsc)
                        wait_chunk(pool, C3["z"], head_num(it, h, l) - EL)
                        settle(pool, s_dsc)
                        nc.gpsimd.tensor_tensor(rows(A[l]), rows(H[l]), weight_head(aself, it, l, h), ALU.mult)\
                          .then_inc(C3["h"].sem, 1)

        def heads_vector(dve, k):
            v = nc.vector
            v.memset(carry[:, :], 0.0).then_inc(s_cz, 1)
            cz[0] += 1
            dve.wait_ge(s_cz, cz[0])
            with dve.Fori(0, EIT) as it:
                for h in range(HEADS):
                    for l in range(EL):
                        n = head_num(it, h, l)
                        if h == 0:
                            dve.wait_ge(s_in[l], landed("load", "heads", 0, it))
                        wait_chunk(dve, C3["t"], n - EL)
                        v.tensor_tensor(rows(B[l]), rows(G[l]), weight_head(alpha, it, l, h), ALU.mult)\
                         .then_inc(C3["g"].sem, 1)
                    for l in range(EL):
                        n = head_num(it, h, l)
                        wait_chunk(dve, C3["g"], n)
                        wait_chunk(dve, C3["h"], n)
                        v.tensor_tensor(B[l], B[l], A[l], ALU.add).then_inc(C3["sum"].sem, 1)
                    for l in range(EL):
                        n = head_num(it, h, l)
                        wait_chunk(dve, C3["carry"], n - 1)
                        wait_chunk(dve, C3["t"], n)
                        v.tensor_tensor_scan(A[l], same[:, bass.ds(at(it, l), CH)], bank[l % 3][:, :],
                                             carry[:, h:h + 1], ALU.mult, ALU.add).then_inc(C3["v"].sem, 1)
                for l in range(EL):
                    wait_chunk(dve, C3["z"], head_num(it, HEADS - 1, l))
                    put_state(dve, bank[3 + l][:, :], it, l, C3["state"])

        def heads_scalar(act, k):
            with act.Fori(0, EIT) as it:
                for h in range(HEADS):
                    for l in range(EL):
                        wait_chunk(act, C3["v"], head_num(it, h, l))
                        nc.scalar.activation(carry[:, h:h + 1], A[l][:, CH - 1:CH], ACT.Copy)\
                          .then_inc(C3["carry"].sem, 1)

        def heads_tensor(pe, k):
            with pe.Fori(0, EIT) as it:
                for h in range(HEADS):
                    for l in range(EL):
                        n = head_num(it, h, l)
                        wait_chunk(pe, C3["sum"], n)
                        wait_chunk(pe, C3["v"], n - 2)
                        transpose4(B[l], bank[l % 3]).then_inc(C3["t"].sem, 1)
                    for l in range(EL):
                        n = head_num(it, h, l)
                        wait_chunk(pe, C3["carry"], n)
                        if h == 0:
                            wait_chunk(pe, C3["state"], num(0, it, l) - EL)
                        nc.tensor.matmul(bank[3 + l][:, :], mats[f"q{h}"][:, :], A[l], start=(h == 0),
                                         stop=(h == HEADS - 1)).then_inc(C3["z"].sem, 1)

        ORDER = FULL_ORDER[:STOP]
        cz = [1]

        @block.sync
        def _(sp):
            setup_sync(sp)
            end_phase(sp)
            dense_sync(sp)
            end_phase(sp, not ORDER)
            run = dict(first=first_sync, tail=tail_sync, spread=spread_sync, scores2=scores2_sync, scores4=scores4_sync,
                       weights=weights_sync, combine=combine_sync, mean=mean_sync, heads=heads_sync)
            for i, (phase, k) in enumerate(ORDER):
                run[phase](sp, k)
                end_phase(sp, i == len(ORDER) - 1)

        @block.gpsimd
        def _(pool):
            setup_pool(pool)
            end_phase(pool)
            map_pool(pool)
            end_phase(pool, not ORDER)
            run = dict(first=first_pool, tail=tail_pool, spread=spread_pool, scores2=scores2_pool, scores4=scores4_pool,
                       weights=weights_pool, combine=combine_pool, mean=mean_pool, heads=heads_pool)
            for i, (phase, k) in enumerate(ORDER):
                run[phase](pool, k)
                end_phase(pool, i == len(ORDER) - 1)

        @block.scalar
        def _(act):
            setup_scalar(act)
            end_phase(act)
            dense_scalar(act)
            end_phase(act, not ORDER)
            run = dict(first=first_scalar, tail=tail_scalar, spread=spread_scalar, scores2=scores2_scalar,
                       scores4=scores4_scalar, weights=weights_scalar, combine=combine_scalar, mean=mean_scalar,
                       heads=heads_scalar)
            for i, (phase, k) in enumerate(ORDER):
                run[phase](act, k)
                end_phase(act, i == len(ORDER) - 1)

        @block.vector
        def _(dve):
            setup_vector(dve)
            end_phase(dve)
            dense_vector(dve)
            end_phase(dve, not ORDER)
            run = dict(first=first_vector, tail=tail_vector, spread=spread_vector, scores2=scores2_vector,
                       scores4=scores4_vector, weights=weights_vector, combine=combine_vector, mean=mean_vector,
                       heads=heads_vector)
            for i, (phase, k) in enumerate(ORDER):
                run[phase](dve, k)
                end_phase(dve, i == len(ORDER) - 1)

        @block.tensor
        def _(pe):
            setup_tensor(pe)
            end_phase(pe)
            dense_tensor(pe)
            end_phase(pe, not ORDER)
            run = dict(first=first_tensor, tail=tail_tensor, spread=spread_tensor, scores2=scores2_tensor,
                       scores4=scores4_tensor, weights=weights_tensor, combine=combine_tensor, mean=mean_tensor,
                       heads=heads_tensor)
            for i, (phase, k) in enumerate(ORDER):
                run[phase](pe, k)
                end_phase(pe, i == len(ORDER) - 1)


_WEIGHTS = ["L0_gnn_Wm", "L0_gnn_bm", "L0_gnn_W1", "L0_gnn_b1", "L0_gnn_W2", "L0_gnn_b2", "L1_gnn_W_src", "L1_gnn_W_dst",
            "L1_gnn_att", "L1_gnn_bias", "L2_gnn_weight", "L2_gnn_bias", "L3_gnn_W1", "L3_gnn_as1", "L3_gnn_ad1",
            "L3_gnn_b1", "L3_gnn_W2", "L3_gnn_as2", "L3_gnn_ad2", "L3_gnn_b2", "L3_gnn_W3", "L3_gnn_as3", "L3_gnn_ad3",
            "L3_gnn_b3"]


def kernel(**inputs):
    import numpy as _np
    import concourse.bacc as _bacc
    from concourse.bass_utils import run_bass_kernel_spmd as _run

    nc = _bacc.Bacc("TRN2", target_bir_lowering=False, num_devices=1)
    x = _np.zeros((NP, P), _np.float32)
    x[:N] = inputs["x"]
    src = _np.zeros(EP, _np.int32)
    src[:E] = inputs["src"]
    dst_all = _np.full(EP + 2, N, _np.int32)
    dst_all[0], dst_all[EP + 1] = -1, -1
    dst_all[1:E + 1] = inputs["dst"]
    ew = _np.zeros(EP, _np.float32)
    ew[:E] = inputs["edge_weight"]

    def by_tile(v):
        return _np.ascontiguousarray(v.reshape(NT, P).T)

    arrays = {"x": x, "src_col": by_tile(src), "dst_col": by_tile(dst_all[1:EP + 1]), "nxt_col": by_tile(dst_all[2:]),
              "dst_all": dst_all, "ew": ew}
    for name in _WEIGHTS:
        arrays[name] = _np.ascontiguousarray(inputs[name])
    args = {k: nc.dram_tensor("in_" + k, v.shape, mybir.dt.from_np(v.dtype), kind="ExternalInput").ap()
            for k, v in arrays.items()}
    out = nc.dram_tensor("out_0", (NP, P), F32, kind="ExternalOutput").ap()
    build(nc, args, out, DEBUG)
    r = _run(nc, [{"in_" + k: v for k, v in arrays.items()}], core_ids=[0])
    return r.results[0]["out_0"][:N]
```

```python
import concourse.bass as bass
from concourse import mybir
from contextlib import ExitStack

F32 = mybir.dt.float32
I32 = mybir.dt.int32
U8 = mybir.dt.uint8
BF16 = mybir.dt.bfloat16
ALU = mybir.AluOpType
ACT = mybir.ActivationFunctionType

P = 128
N, E = 50000, 25000
CH = 512
TILES = CH // P
DL, EL = 5, 5
NCH = -(-N // (CH * DL)) * DL
ECH = -(-E // (CH * EL)) * EL
NP, EP = NCH * CH, ECH * CH
DIT, EIT = NCH // DL, ECH // EL
NT = EP // P
RP = NT // 2
TAB = NP + EP
HEADS = 4
PARTS = 3
EPS = 1e-5
SLOPE = 0.2
FAR = float(1 << 20)
NEG = -3.0e38
CREDIT = 2 * EL
ENGINES = 5


class Stage:

    def __init__(self, sem):
        self.sem = sem

    def done(self, n):
        return n + (CREDIT + 1)


class Pass:

    def __init__(self, sems, index, per_round):
        self.sems, self.index, self.per_round = sems, index, per_round

    def wait(self, eng, it, lane):
        eng.wait_ge(self.sems[lane], it * self.per_round + (self.per_round + self.index + 1))

    def wait_before(self, eng, it, lane):
        eng.wait_ge(self.sems[lane], it * self.per_round + (self.index + 1))


DENSE_STEPS = [step.split(":") for step in (
    "tensor:t0:8 scalar:f0:9 tensor:m0:12 scalar:f1:9 tensor:r0:15 vector:y0:13 "
    "vector:st0:15 vector:var0:10 scalar:sd0:6 vector:rs0:8 vector:out0:17 sync:z:0 "
    "tensor:t1:8 scalar:f0b:9 tensor:r1:13 sync:stored:0 scalar:xs0:10 tensor:t2:8 scalar:f1b:9 tensor:r2:13 scalar:xs1:10 sync:xs0:0 "
    "tensor:t3:8 scalar:f0c:9 tensor:r3:13 scalar:xs2:10 sync:xs1:0 vector:ya:13 vector:y1:13 sync:xs2:0 "
    "vector:st1:15 vector:var1:10 scalar:sd1:6 vector:rs1:8 vector:out1:17 sync:x4:0 "
    "tensor:t4:8 scalar:f1c:9 tensor:r4:15 vector:y2:13 vector:st2:15 vector:var2:10 scalar:sd2:6 vector:rs2:8 vector:out2:17 "
    "tensor:t5:8 scalar:f0d:9 tensor:r5:13 scalar:p5:10 tensor:t6:8 scalar:f1d:9 tensor:r6:13 scalar:p6:10 sync:p5:0 "
    "tensor:t7:8 scalar:f0e:9 tensor:t8:8 scalar:x7:10 sync:p6:0 tensor:r7:15 sync:x7:0 vector:y3:13 "
    "vector:st3:15 vector:var3:10 scalar:sd3:6 vector:rs3:8 vector:out3:17 sync:xo:0").split()]
DENSE_ROUND = 589


def dense_schedule(engine):
    steps = []
    for lane in range(DL):
        time = lane * DENSE_ROUND // DL
        for eng, name, takes in DENSE_STEPS:
            if eng == engine:
                steps.append((time % DENSE_ROUND, time // DENSE_ROUND, lane, name))
            time += int(takes)
    return sorted(steps, key=lambda step: step[0])


def build(nc, a, out):
    ctx = ExitStack()
    with ctx:
        def sb(name, shape, dt=F32):
            return ctx.enter_context(nc.sbuf_tensor(name, shape, dt))

        def sem(name):
            return ctx.enter_context(nc.semaphore(name))

        def dram(name, shape, dt=F32):
            return nc.dram_tensor(name, shape, dt, kind="Internal").ap()

        node_row = dram("node_row", [NP, 1], I32)
        table = [None] + [dram(f"table{i}", [TAB, P]) for i in range(1, 8)]
        own = {0: dram("own0", [EP, P]), 1: dram("own1", [EP, P]), 5: dram("own5", [EP, P])}
        staged = dram("staged", [EP, P])
        scores = dram("scores", [2 * HEADS, EP])

        work = sb("work", [P, EP + 4 * EL * CH])
        state = work[:, 0:EP]

        def lane_buffers(at, lanes):
            return [work[:, at + l * CH:at + (l + 1) * CH] for l in range(lanes)]

        G, H, A, B = [lane_buffers(EP + i * EL * CH, EL) for i in range(4)]
        names = "z f0 f1 y x1 xs0 xs1 xs2 x4 p5 p6 x7 xo".split()
        d = {nm: lane_buffers(i * DL * CH, DL) for i, nm in enumerate(names)}
        assert len(names) * DL * CH <= EP + 3 * EL * CH
        d["x5"] = d["x1"]

        def rows(buf):
            return buf.rearrange("p (j f) -> p j f", j=TILES)

        same = sb("same", [P, EP + 1], U8)
        ident = sb("ident", [P, P])
        one = sb("one", [1, 1])
        gather_row = sb("gather_row", [P, NT], I32)
        src_col = sb("src_col", [P, NT], I32)
        dst_col = sb("dst_col", [P, NT], I32)
        last_row = sb("last_row", [P, NT], I32)
        idx = [sb(f"idx{l}", [P, TILES], I32) for l in range(EL)]
        idx2 = [sb(f"idx2{l}", [P, TILES], I32) for l in range(EL)]
        shared = sb("shared", [P, EL * CH])
        ew = shared[0:1, :]
        alpha = shared[:, 0:NT * HEADS]
        aself = shared[:, NT * HEADS:2 * NT * HEADS]
        alpha4 = alpha[:, :].rearrange("p (t h) -> p t h", h=HEADS)
        aself4 = aself[:, :].rearrange("p (t h) -> p t h", h=HEADS)
        mean_w = sb("mean_w", [P, NT])
        nxt_col = alpha[:, 0:NT].bitcast(I32)
        slot_row = alpha[:, NT:2 * NT].bitcast(I32)
        lastf = alpha[:, 2 * NT:3 * NT]
        mats = {nm: sb(nm, [P, P]) for nm in
                "Wd0 Ws0 W1a W1b W2 Wz gS0 gS1 gS2 gD0 gD1 gD2 gB0 gB1 gB2 Wa Wx V1 V2 q0 q1 q2 q3 V3m".split()}
        c = {nm: sb("c_" + nm, [P, 1]) for nm in "bm b1 bz gb0 gb1 gb2 att0 att1 att2 natt0 natt1 natt2 vb1 vb2".split()}
        bc = {"gb2": sb("bc_gb2", [P, P])}
        bias3 = {nm: sb("bias_" + nm, [PARTS * 32, P], BF16) for nm in "b2 l2 b3".split()}
        ones3 = sb("ones3", [PARTS * 32, P], BF16)
        ww = sb("ww", [1, P])
        asd = {k: sb(f"asd{k}", [P, 2 * HEADS]) for k in (1, 2, 3)}
        src8 = {k: sb(f"src8{k}", [P, 2 * HEADS]) for k in (1, 2, 3)}
        dst8 = {k: sb(f"dst8{k}", [P, 2 * HEADS]) for k in (1, 2, 3)}
        block_mask = sb("block_mask", [P, HEADS])
        st = sb("st", [P, EL, TILES, 6])
        mv = sb("mv", [P, EL, TILES, 2])
        sd = sb("sd", [P, EL, TILES])
        rs = sb("rs", [P, EL, TILES])
        carry = sb("carry", [P, HEADS])
        eps = sb("eps", [P, 1])
        root = sb("root", [P, 1])
        score_rows = [shared[0:2 * HEADS, l * CH:(l + 1) * CH] for l in range(EL)]
        names_r = "cont contb contz contbz pre suf end".split()
        R = {nm: sb("r_" + nm, [RP, 2 * P]) for nm in names_r}
        frow = sb("frow", [1, 2 * NT])
        erow = sb("erow", [1, 2 * NT + 2])
        ccol = sb("ccol", [RP, 4])

        def tmp(i):
            return work[0:RP, EP + i * 2 * P:EP + (i + 1) * 2 * P]

        T = {nm: tmp(i) for i, nm in enumerate("e s d f b t m w c u di dm".split())}
        bank = [ctx.enter_context(nc.psum_tensor(f"bank{i}", [P, CH], F32)) for i in range(8)]


        def stages(text):
            return {nm: Stage(sem(nm)) for nm in text.split()}

        all_stages = []

        def stage_set(prefix, text):
            got = {nm: Stage(sem(prefix + nm)) for nm in text.split()}
            all_stages.extend(got.values())
            return got

        D = {}
        for engine in ("tensor", "scalar", "vector", "sync"):
            names_ = [name for eng, name, _ in DENSE_STEPS if eng == engine]
            if engine == "sync":
                names_ = ["stored"]
            lane_sems_ = [sem(f"dense_{engine}{l}") for l in range(DL)]
            D.update({nm: Pass(lane_sems_, i, len(names_)) for i, nm in enumerate(names_)})
        LNS = stage_set("sn_", "st var sd rs out")
        E0 = stage_set("e_", "gT a hT s m neg scan h r last")
        GA = stage_set("g_", "idx pre a self b la lb e row stored")
        LA = stage_set("l_", "idx gT a e row stored")
        CA = stage_set("c_", "g h t v relu r rows state last stored")
        CM = stage_set("m_", "idx g t v c last stored")
        C3 = stage_set("h_", "g h sum t v carry z")
        TL = stage_set("t_", "o y xt x r g state idx")
        s_spread = sem("spread")
        s_phase = sem("phase")
        s_pool = sem("pool_settled")
        s_dve = sem("vector_settled")
        s_w = sem("weights")
        s_const = sem("const")
        s_set, s_setp, s_seta = sem("setup_vector"), sem("setup_tensor"), sem("setup_scalar")
        s_mask, s_map = sem("mask"), sem("map")
        s_vs, s_ts, s_as, s_ds = sem("seg_vector"), sem("seg_tensor"), sem("seg_scalar"), sem("seg_load")

        def lane_sems(name, lanes):
            return [sem(f"{name}{l}") for l in range(lanes)]

        s_z = lane_sems("z_loaded", DL)
        s_zo = lane_sems("dense_store", DL)
        s_in = lane_sems("load", EL)
        s_in2 = lane_sems("load_own", EL)
        s_ew = lane_sems("edge_weights", EL)
        s_ga = lane_sems("gathered", EL)
        s_gb = lane_sems("gathered_dst", EL)
        s_mk = lane_sems("mask_load", 2)
        s_out = lane_sems("scattered", EL)
        s_dsc, s_sc, s_sc2, s_gr = sem("pool_step"), sem("map_scattered"), sem("map_gathered"), sem("gather_rows")
        s_sync = sem("sync_step")
        s_zg, s_zs = sem("x_gathered"), sem("x_stored")
        s_settle, s_cz = sem("vector_step"), sem("carry_cleared")
        s_st = lane_sems("store", EL)
        block = ctx.enter_context(nc.Block())

        def at(it, lane):
            return it * (EL * CH) + lane * CH

        def at_back(it, lane):
            return (ECH - 1) * CH - lane * CH - it * (EL * CH)

        def num(use, it, lane):
            return use * ECH + it * EL + lane

        def slot_rows(tensor, start, base=0):
            return tensor[bass.ds(base + start, CH), :].rearrange("(j p) f -> p j f", p=P)

        phase_no = {}

        def end_phase(eng, last=False):
            phase_no[eng.engine] = phase_no.get(eng.engine, 0) + 1
            eng.drain().then_inc(s_phase, 1)
            if not last:
                eng.wait_ge(s_phase, ENGINES * phase_no[eng.engine])
                eng.nop()

        def settle(eng, s):
            eng.sem_inc(s, 1)

        def transpose4(src, dst, **kw):
            for j in range(TILES):
                ins = nc.tensor.transpose(dst[:, j * P:(j + 1) * P], src[:, j * P:(j + 1) * P], ident[:, :])
            return ins

        def rows4(src, mat, dst):
            for j in range(TILES):
                ins = nc.tensor.matmul(dst[:, j * P:(j + 1) * P], src[:, j * P:(j + 1) * P], mat[:, :],
                                       start=True, stop=True)
            return ins

        def bias_rows(nm, dst):
            four = bias3[nm][:, :].unsqueeze(1).to_broadcast([PARTS * 32, TILES, P])
            nc.tensor.matmul(dst.rearrange("p (j f) -> p j f", j=TILES), ones3[:, :], four, start=True, stop=False)

        def rows4_add(src, mat, dst, stop):
            for j in range(TILES):
                ins = nc.tensor.matmul(dst[:, j * P:(j + 1) * P], src[:, j * P:(j + 1) * P], mat[:, :],
                                       start=False, stop=stop and j == TILES - 1)
            return ins

        tmp_a, tmp_x = work[:, 0:P], work[:, P:2 * P]
        V3 = work[:, 2 * P:2 * P + HEADS * P]
        asc = {k: work[:, 6 * P + 2 * k:6 * P + 2 * k + 2] for k in (1, 2)}
        comb = {k: work[:, 6 * P + 16 + 8 * k:6 * P + 24 + 8 * k] for k in (1, 2, 3)}
        turned = work[:, 7 * P:16 * P]
        tcol = work[:, 16 * P:16 * P + NT]
        brow = {nm: work[0:PARTS * 32, (19 + i) * P:(20 + i) * P] for i, nm in enumerate(("b2", "l2", "b3"))}
        bpart = work[0:PARTS * 32, 22 * P:22 * P + P // 2].bitcast(BF16)
        MB = EP // 10
        mbuf = [work[:, 4096 + l * 2816:4096 + l * 2816 + MB + 1].bitcast(I32) for l in range(2)]
        node_iota = work[:, 10000:10000 + NP // P].bitcast(I32)
        dR, pR, nR = (tmp(i).bitcast(I32) for i in range(3))

        def compact(v):
            return v.rearrange("(g q i) -> q g i", g=2, i=P)

        def compact_sb(v):
            return v.rearrange("q (g i) -> q g i", g=2)

        def column(v):
            return v.rearrange("(p o) -> p o", o=1)

        loads = [(mats["Wd0"][:, :], a["L0_gnn_Wm"][0:P, :]), (mats["Ws0"][:, :], a["L0_gnn_Wm"][P:2 * P, :]),
                 (ww[:, :], a["L0_gnn_Wm"][2 * P:2 * P + 1, :]),
                 (mats["W1a"][:, :], a["L0_gnn_W1"][0:P, :]), (mats["W1b"][:, :], a["L0_gnn_W1"][P:2 * P, :]),
                 (mats["W2"][:, :], a["L0_gnn_W2"][:, :]),
                 (tmp_a, a["L2_gnn_weight"][:, 0:P]), (tmp_x, a["L2_gnn_weight"][:, P:2 * P]),
                 (mats["V1"][:, :], a["L3_gnn_W1"][:, :]), (mats["V2"][:, :], a["L3_gnn_W2"][:, :]),
                 (V3, a["L3_gnn_W3"][:, :]),
                 (c["bm"][:, :], column(a["L0_gnn_bm"])), (c["b1"][:, :], column(a["L0_gnn_b1"])),
                 (c["vb1"][:, :], column(a["L3_gnn_b1"])), (c["vb2"][:, :], column(a["L3_gnn_b2"]))]
        for l in range(3):
            loads += [(mats[f"gS{l}"][:, :], a["L1_gnn_W_src"][l]), (mats[f"gD{l}"][:, :], a["L1_gnn_W_dst"][l]),
                      (c[f"gb{l}"][:, :], column(a["L1_gnn_bias"][l])), (c[f"att{l}"][:, :], column(a["L1_gnn_att"][l]))]
        loads.append((bc["gb2"][:, :], a["L1_gnn_bias"][2].partition_broadcast(P)))
        for nm, v in (("b2", a["L0_gnn_b2"]), ("l2", a["L2_gnn_bias"]), ("b3", a["L3_gnn_b3"])):
            loads.append((brow[nm], v.partition_broadcast(PARTS * 32)))
        for k in (1, 2):
            loads += [(asc[k][:, 0:1], a[f"L3_gnn_as{k}"].rearrange("h (c o) -> (h c) o", o=1)),
                      (asc[k][:, 1:2], a[f"L3_gnn_ad{k}"].rearrange("h (c o) -> (h c) o", o=1))]
        loads += [(asd[3][:, 0:HEADS], a["L3_gnn_as3"].rearrange("h c -> c h")),
                  (asd[3][:, HEADS:], a["L3_gnn_ad3"].rearrange("h c -> c h"))]
        col_loads = [(src_col[:, :], a["src_col"]), (dst_col[:, :], a["dst_col"]), (nxt_col, a["nxt_col"]),
                     (compact_sb(dR), compact(a["dst_all"][1:1 + EP])), (compact_sb(pR), compact(a["dst_all"][0:EP])),
                     (compact_sb(nR), compact(a["dst_all"][2:2 + EP]))]
        mask_stage = Stage(s_mask)

        def setup_sync(sp):
            for dst, src in col_loads:
                sp.dma_start(dst, src).then_inc(s_const, 16)
            with nc.allow_non_contiguous_dma(reason="1024 elements of the last layer's attention vectors"):
                for dst, src in loads:
                    sp.dma_start(dst, src).then_inc(s_w, 16)
            with sp.Fori(0, 5) as it:
                for l in range(2):
                    sp.wait_ge(s_mask, mask_stage.done(it * 2 + l) - 2)
                    settle(sp, s_sync)
                    sp.dma_start(mbuf[l], a["dst_all"][bass.ds(it * (2 * MB) + l * MB, MB + 1)].partition_broadcast(P))\
                      .then_inc(s_mk[l], 16)

        def chain(eng, s):
            n = [0]

            def link(ins):
                n[0] += 1
                ins.then_inc(s, 1)
                eng.wait_ge(s, n[0])
            return link

        def setup_vector(dve):
            v = nc.vector
            link = chain(dve, s_dve)
            dve.sem_inc(s_mask, CREDIT)
            for stage in all_stages:
                dve.sem_inc(stage.sem, CREDIT)
            for l in range(EL):
                dve.sem_inc(s_st[l], 16)
            for nm in ("t0", "f0", "y0", "stored"):
                for l in range(DL):
                    dve.sem_inc(D[nm].sems[l], D[nm].per_round)
            for l in range(DL):
                dve.sem_inc(s_zo[l], 16)
            link(v.memset(same[:, EP:EP + 1], 0))
            link(v.memset(one[:, :], 1.0))
            link(v.memset(eps[:, :], EPS))
            link(v.memset(block_mask[:, :], 0.0))
            link(v.memset(erow[:, :], 0.0))
            for h in range(HEADS):
                link(v.memset(block_mask[32 * h:32 * h + 32, h:h + 1], 1.0))
            for k in (1, 2, 3):
                link(v.memset(src8[k][:, :], 0.0))
            dve.wait_ge(s_const, 16 * len(col_loads))
            link(v.tensor_tensor(lastf, dst_col[:, :], nxt_col, ALU.not_equal))
            link(v.scalar_tensor_tensor(tcol, dst_col[:, :], FAR, lastf, ALU.subtract, ALU.mult))
            link(v.tensor_scalar(last_row[:, :], tcol, FAR, None, ALU.add))
            v.tensor_copy(tcol[:, 0:1], tcol[:, 1:2]).then_inc(s_map, 1)
            link(v.tensor_tensor(R["cont"][:, :], dR, pR, ALU.is_equal))
            link(v.tensor_tensor(R["contb"][:, :], dR, nR, ALU.is_equal))
            link(v.tensor_scalar(R["end"][:, :], R["contb"][:, :], -1.0, 1.0, ALU.mult, ALU.add))
            link(v.tensor_copy(R["contz"][:, :], R["cont"][:, :]))
            link(v.tensor_copy(R["contbz"][:, :], R["contb"][:, :]))
            for g in range(2):
                link(v.memset(R["contz"][:, g * P:g * P + 1], 0.0))
                link(v.memset(R["contbz"][:, g * P + P - 1:g * P + P], 0.0))
                cg, bg = R["cont"][:, g * P:(g + 1) * P], R["contb"][:, g * P:(g + 1) * P]
                link(v.tensor_tensor_scan(R["pre"][:, g * P:(g + 1) * P], cg, cg, 1.0, ALU.min, ALU.min))
                link(v.tensor_tensor_scan(R["suf"][:, g * P:(g + 1) * P][:, ::-1], bg[:, ::-1], bg[:, ::-1], 1.0,
                                          ALU.min, ALU.min))
            v.tensor_copy(tcol[:, 0:1], tcol[:, 1:2]).then_inc(s_set, 1)
            dve.wait_ge(s_w, 16 * len(loads))
            for k in (1, 2):
                link(v.tensor_scalar(asd[k][:, 0:HEADS], block_mask[:, :], asc[k][:, 0:1], None, ALU.mult))
                link(v.tensor_scalar(asd[k][:, HEADS:], block_mask[:, :], asc[k][:, 1:2], None, ALU.mult))
                link(v.tensor_copy(src8[k][:, 0:HEADS], asd[k][:, 0:HEADS]))
            for k in (1, 2, 3):
                link(v.tensor_copy(comb[k][:, 0:HEADS], asd[k][:, HEADS:]))
                link(v.tensor_tensor(comb[k][:, HEADS:], asd[k][:, 0:HEADS], asd[k][:, HEADS:], ALU.add))
            link(v.memset(ones3[:, :], 1.0))
            for nm in ("b2", "l2", "b3"):
                link(v.memset(bias3[nm][:, :], 0.0))
                for i in range(PARTS):
                    link(v.tensor_copy(bpart, brow[nm]))
                    link(v.tensor_copy(bias3[nm][32 * i:32 * i + 1, :], bpart[32 * i:32 * i + 1, :]))
                    link(v.tensor_tensor(brow[nm], brow[nm], bpart, ALU.subtract))
            for l in range(3):
                link(v.tensor_tensor(mats[f"gB{l}"][:, :], mats[f"gS{l}"][:, :], mats[f"gD{l}"][:, :], ALU.add))
                link(v.tensor_scalar(c[f"natt{l}"][:, :], c[f"att{l}"][:, :], -1.0, None, ALU.mult))
            for h in range(HEADS):
                link(v.tensor_scalar(mats[f"q{h}"][:, :], V3[:, h * P:(h + 1) * P], 1.0 / HEADS, None, ALU.mult))
            link(v.tensor_tensor(mats["V3m"][:, :], mats["q0"][:, :], mats["q1"][:, :], ALU.add))
            link(v.tensor_tensor(mats["V3m"][:, :], mats["V3m"][:, :], mats["q2"][:, :], ALU.add))
            link(v.tensor_tensor(mats["V3m"][:, :], mats["V3m"][:, :], mats["q3"][:, :], ALU.add))
            dve.wait_ge(s_setp, 1)
            for i in range(3):
                w = min(CH, 9 * P - i * CH)
                link(v.tensor_copy(turned[:, i * CH:i * CH + w], bank[i][:, 0:w]))
            link(v.tensor_copy(mats["Wa"][:, :], turned[:, 0:P]))
            link(v.tensor_copy(mats["Wx"][:, :], turned[:, P:2 * P]))
            v.tensor_copy(tcol[:, 0:1], tcol[:, 1:2]).then_inc(s_set, 1)
            dve.wait_ge(s_setp, 2)
            b3 = bank[3]
            link(v.tensor_tensor(mats["Wz"][:, :], b3[:, 0:P], mats["W1a"][:, :], ALU.add))
            link(v.tensor_tensor(c["bz"][:, :], b3[:, P:P + 1], c["b1"][:, :], ALU.add))
            for k in (1, 2):
                link(v.tensor_copy(dst8[k][:, :], b3[:, P + 8 * k:P + 8 * k + 8]))
            for h in range(HEADS):
                link(v.tensor_copy(src8[3][:, h:h + 1], b3[:, P + 32 + 2 * h:P + 33 + 2 * h]))
                link(v.tensor_copy(dst8[3][:, h:h + 1], b3[:, P + 33 + 2 * h:P + 34 + 2 * h]))
            link(v.tensor_tensor(dst8[3][:, HEADS:], src8[3][:, 0:HEADS], dst8[3][:, 0:HEADS], ALU.add))
            dve.wait_ge(s_setp, 3)
            link(v.tensor_copy(frow[:, :], bank[4][0:1, 0:2 * NT]))
            with dve.Fori(0, 5) as it:
                for l in range(2):
                    dve.wait_ge(s_mk[l], it * 16 + 16)
                    v.tensor_tensor(same[:, bass.ds(it * (2 * MB) + l * MB, MB)], mbuf[l][:, 1:MB + 1],
                                    mbuf[l][:, 0:MB], ALU.is_equal).then_inc(s_mask, 1)

        def setup_tensor(pe):
            t = nc.tensor
            pe.wait_ge(s_seta, 2)
            pe.wait_ge(s_w, 16 * len(loads))
            sources = [tmp_a, tmp_x, mats["Wd0"][:, :], mats["V1"][:, :], mats["V2"][:, :]] + \
                      [V3[:, h * P:(h + 1) * P] for h in range(HEADS)]
            for i, m in enumerate(sources):
                last = t.transpose(bank[i // 4][:, (i % 4) * P:(i % 4 + 1) * P], m, ident[:, :])
            last.then_inc(s_setp, 1)
            pe.wait_ge(s_set, 2)
            b3 = bank[3]

            def T_(i):
                return turned[:, i * P:(i + 1) * P]

            t.matmul(b3[:, 0:P], T_(2), mats["W1b"][:, :], start=True, stop=True)
            t.matmul(b3[:, P:P + 1], mats["W1b"][:, :], c["bm"][:, :], start=True, stop=True)
            for k in (1, 2):
                t.matmul(b3[:, P + 8 * k:P + 8 * k + 8], T_(2 + k), comb[k][:, :], start=True, stop=True)
            for h in range(HEADS):
                last = t.matmul(b3[:, P + 32 + 2 * h:P + 34 + 2 * h], T_(5 + h), asd[3][:, h::HEADS], start=True, stop=True)
            last.then_inc(s_setp, 1)
            pe.wait_ge(s_set, 1)
            for i, (m, col) in enumerate((("pre", P - 1), ("pre", 2 * P - 1), ("suf", 0), ("suf", P))):
                last = t.transpose(bank[4][0:1, i * RP:(i + 1) * RP], R[m][:, col:col + 1], ident[0:RP, 0:RP])
            last.then_inc(s_setp, 1)

        def setup_scalar(act):
            pass

        def setup_pool(pool):
            g = nc.gpsimd
            g.memset(ident[:, :], 0.0).then_inc(s_seta, 1)
            pool.wait_ge(s_seta, 1)
            g.affine_select(out=ident[:, :], in_=ident[:, :], compare_op=ALU.not_equal, fill=1.0, base=0,
                            pattern=[[-1, P]], channel_multiplier=1).then_inc(s_seta, 1)
            g.iota(slot_row, pattern=[[P, NT]], base=NP, channel_multiplier=1).then_inc(s_seta, 1)
            g.iota(node_iota, pattern=[[1, NP // P]], base=0, channel_multiplier=NP // P).then_inc(s_seta, 1)
            pool.wait_ge(s_seta, 4)
            pool.dma_start(node_row.rearrange("(p j) o -> p (j o)", p=P), node_iota).then_inc(s_sc, 16)
            pool.wait_ge(s_sc, 16)
            pool.wait_ge(s_map, 1)

        def map_pool(pool):
            g = nc.gpsimd
            with pool.Fori(0, EIT) as it:
                for l in range(EL):
                    g.tensor_copy(idx[l][:, :], last_row[:, bass.ds(it * (EL * TILES) + l * TILES, TILES)])
                    g.tensor_copy(idx2[l][:, :], slot_row[:, bass.ds(it * (EL * TILES) + l * TILES, TILES)])\
                     .then_inc(s_pool, 1)
                pool.wait_ge(s_pool, it * EL + EL)
                settle(pool, s_dsc)
                for l in range(EL):
                    for j in range(TILES):
                        pool.indirect_dma_start(node_row, bass.IndirectOffsetOnAxis(ap=idx[l][:, j:j + 1], axis=0),
                                                idx2[l][:, j:j + 1], None, bounds_check=NP - 1,
                                                oob_is_err=False).then_inc(s_sc, 16)
                pool.wait_ge(s_sc, it * (16 * EL * TILES) + (16 * EL * TILES + 16))
                settle(pool, s_dsc)
            with pool.Fori(0, EIT) as it:
                for l in range(EL):
                    g.tensor_copy(idx[l][:, :], src_col[:, bass.ds(it * (EL * TILES) + l * TILES, TILES)])\
                     .then_inc(s_pool, 1)
                pool.wait_ge(s_pool, it * EL + (EL * EIT + EL))
                settle(pool, s_dsc)
                for l in range(EL):
                    for j in range(TILES):
                        pool.indirect_dma_start(idx2[l][:, j:j + 1], None, node_row,
                                                bass.IndirectOffsetOnAxis(ap=idx[l][:, j:j + 1], axis=0))\
                            .then_inc(s_sc2, 16)
                pool.wait_ge(s_sc2, it * (16 * EL * TILES) + 16 * EL * TILES)
                settle(pool, s_dsc)
                for l in range(EL):
                    last = g.tensor_copy(gather_row[:, bass.ds(it * (EL * TILES) + l * TILES, TILES)], idx2[l][:, :])
                last.then_inc(s_gr, 1)
                pool.wait_ge(s_gr, it + 1)
                settle(pool, s_dsc)
            for i, (cols, target) in enumerate(((src_col, staged), (dst_col, own[0]))):
                with pool.Fori(0, EIT) as it:
                    for l in range(EL):
                        g.tensor_copy(idx[l][:, :], cols[:, bass.ds(it * (EL * TILES) + l * TILES, TILES)])\
                         .then_inc(s_pool, 1)
                    pool.wait_ge(s_pool, it * EL + ((2 + i) * EL * EIT + EL))
                    settle(pool, s_dsc)
                    for l in range(EL):
                        for j in range(TILES):
                            pool.indirect_dma_start(rows(B[l])[:, j, :], None, a["x"],
                                                    bass.IndirectOffsetOnAxis(ap=idx[l][:, j:j + 1], axis=0))\
                                .then_inc(s_zg, 16)
                    pool.wait_ge(s_zg, it * (16 * EL * TILES) + 16 * EL * TILES * (1 + i * EIT))
                    settle(pool, s_dsc)
                    for l in range(EL):
                        pool.dma_start(slot_rows(target, at(it, l)), rows(B[l])).then_inc(s_zs, 16)
                    pool.wait_ge(s_zs, it * (16 * EL) + 16 * EL * (1 + i * EIT))
                    settle(pool, s_dsc)

        def chunk_rows(tensor, it, lane):
            return tensor[bass.ds(it * (DL * CH) + lane * CH, CH), :].rearrange("(p j) f -> p (j f)", j=TILES)

        def dense_rounds(eng, engine, step):
            schedule = dense_schedule(engine)
            assert all(late <= 1 for _, late, _, _ in schedule)
            for _, late, lane, name in schedule:
                if not late:
                    step(name, 0, lane)
            with eng.Fori(0, DIT - 1) as i:
                for _, late, lane, name in schedule:
                    step(name, i if late else i + 1, lane)
            for _, late, lane, name in schedule:
                if late:
                    step(name, DIT - 1, lane)

        def dense_sync(sp):
            rows_of = {"xs0": ("xs0", table[1]), "xs1": ("xs1", table[2]), "xs2": ("xs2", table[3]), "x4": ("out1", table[4]),
                       "p5": ("p5", table[5]), "p6": ("p6", table[6]), "x7": ("x7", table[7]), "xo": ("out3", out)}

            def step(name, it, l):
                if name == "stored":
                    sp.wait_ge(s_zo[l], it * (16 * 8) + 16)
                    sp.sem_inc(D["stored"].sems[l], 1)
                elif name == "z":
                    D["y0"].wait(sp, it, l)
                    settle(sp, s_sync)
                    D["t0"].wait(sp, it, l)
                    settle(sp, s_sync)
                    sp.dma_start(d["z"][l], chunk_rows(a["x"], it + 1, l)).then_inc(s_z[l], 16)
                else:
                    ready, target = rows_of[name]
                    D[ready].wait(sp, it, l)
                    settle(sp, s_sync)
                    sp.dma_start(chunk_rows(target, it, l), d[name][l]).then_inc(s_zo[l], 16)

            for l in range(DL):
                sp.dma_start(d["z"][l], chunk_rows(a["x"], 0, l)).then_inc(s_z[l], 16)
            dense_rounds(sp, "sync", step)
            for l in range(DL):
                sp.wait_ge(s_zo[l], DIT * 16 * 8 + 16)
                sp.wait_ge(s_z[l], (DIT + 1) * 16)

        def dense_tensor(pe):
            turns = {"t0": ("z", None), "t1": ("x1", "out0"), "t2": ("xs0", "xs0"), "t3": ("xs1", "xs1"), "t4": ("x4", "out1"),
                     "t5": ("x5", "out2"), "t6": ("p5", "p5"), "t7": ("p6", "p6"), "t8": ("f0", "f0e")}
            products = {"r0": ("f1", "f1", "W2", "b2"), "r1": ("f0", "f0b", "gS0", None), "r2": ("f1", "f1b", "gS1", None),
                        "r3": ("f0", "f0c", "gS2", None), "r4": ("f1", "f1c", "Wx", "l2"), "r5": ("f0", "f0d", "V1", None),
                        "r6": ("f1", "f1d", "V2", None), "r7": ("f0", "x7", "V3m", "b3")}

            def step(name, it, l):
                if name == "m0":
                    D["f0"].wait(pe, it, l)
                    nc.tensor.matmul(bank[l][:, :], mats["W1a"][:, :], d["f0"][l], start=True, stop=True)\
                      .then_inc(D[name].sems[l], 1)
                elif name in turns:
                    buf, ready = turns[name]
                    if ready:
                        D[ready].wait(pe, it, l)
                    else:
                        pe.wait_ge(s_z[l], it * 16 + 16)
                        D["y3"].wait_before(pe, it, l)
                    transpose4(d[buf][l], bank[l]).then_inc(D[name].sems[l], 1)
                else:
                    buf, ready, mat, bias = products[name]
                    D[ready].wait(pe, it, l)
                    if bias:
                        bias_rows(bias, bank[l])
                        rows4_add(d[buf][l], mats[mat], bank[l], True).then_inc(D[name].sems[l], 1)
                    else:
                        rows4(d[buf][l], mats[mat], bank[l]).then_inc(D[name].sems[l], 1)

            dense_rounds(pe, "tensor", step)

        def dense_scalar(act):
            moves = {"f0": ("t0", "f0", None), "f1": ("m0", "f1", "b1"), "f0b": ("t1", "f0", None), "xs0": ("r1", "xs0", None),
                     "f1b": ("t2", "f1", "gb0"), "xs1": ("r2", "xs1", None), "f0c": ("t3", "f0", "gb1"),
                     "xs2": ("r3", "xs2", None), "f1c": ("t4", "f1", None), "f0d": ("t5", "f0", None), "p5": ("r5", "p5", None),
                     "f1d": ("t6", "f1", "vb1"), "p6": ("r6", "p6", None), "f0e": ("t7", "f0", "vb2"), "x7": ("t8", "x7", None)}

            def step(name, it, l):
                if name in moves:
                    ready, buf, bias = moves[name]
                    D[ready].wait(act, it, l)
                    if name == "xs0":
                        D["stored"].wait(act, it, l)
                    if bias:
                        ins = nc.scalar.activation(d[buf][l], bank[l][:, :], ACT.Relu, bias=c[bias][:, :])
                    else:
                        ins = nc.scalar.activation(d[buf][l], bank[l][:, :], ACT.Copy)
                else:
                    D["var" + name[2:]].wait(act, it, l)
                    ins = nc.scalar.activation(sd[:, l, :], mv[:, l, :, 1], ACT.Sqrt, bias=eps[:, :])
                ins.then_inc(D[name].sems[l], 1)

            sqrt_table()
            dense_rounds(act, "scalar", step)

        def sqrt_table():
            nc.scalar.activation(root[:, :], eps[:, :], ACT.Sqrt)

        def norm_scalar(act, LN, lanes, n0):
            for l in range(lanes):
                act.wait_ge(LN["var"].sem, LN["var"].done(n0 + l))
                nc.scalar.activation(sd[:, l, :], mv[:, l, :, 1], ACT.Sqrt, bias=eps[:, :])\
                  .then_inc(LN["sd"].sem, 1)

        def norm_vector(dve, LN, lanes, n0, ready, ready_sem, src, dst):
            v = nc.vector
            for turn in range(lanes + 3):
                l = turn
                if l < lanes:
                    dve.wait_ge(ready_sem, ready(l))
                    for j in range(TILES):
                        last = v.bn_stats(st[:, l, j, :], src[l][:, j * P:(j + 1) * P])
                    last.then_inc(LN["st"].sem, 1)
                l = turn - 1
                if 0 <= l < lanes:
                    dve.wait_ge(LN["st"].sem, LN["st"].done(n0 + l))
                    settle(dve, s_settle)
                    for j in range(TILES):
                        last = v.bn_aggr(mv[:, l, j, :], st[:, l, j, :])
                    last.then_inc(LN["var"].sem, 1)
                l = turn - 2
                if 0 <= l < lanes:
                    dve.wait_ge(LN["sd"].sem, LN["sd"].done(n0 + l))
                    v.reciprocal(rs[:, l, :], sd[:, l, :]).then_inc(LN["rs"].sem, 1)
                l = turn - 3
                if 0 <= l < lanes:
                    dve.wait_ge(LN["rs"].sem, LN["rs"].done(n0 + l))
                    for j in range(TILES):
                        last = v.tensor_scalar(dst[l][:, j * P:(j + 1) * P], src[l][:, j * P:(j + 1) * P],
                                               mv[:, l, j, 0:1], rs[:, l, j:j + 1], ALU.subtract, ALU.mult)
                    last.then_inc(LN["out"].sem, 1)

        def over_rows(vec):
            return vec[:, :].unsqueeze(1).to_broadcast([P, TILES, P])

        def dense_vector(dve):
            v = nc.vector
            normed = ["x1", "x4", "x5", "xo"]

            def step(name, it, l):
                y = d["y"][l]
                if name in ("y0", "y2", "y3"):
                    ready, res = {"y0": ("r0", "z"), "y2": ("r4", "x4"), "y3": ("r7", "x5")}[name]
                    D[ready].wait(dve, it, l)
                    if name == "y0":
                        dve.wait_ge(s_z[l], it * 16 + 16)
                        D["out3"].wait_before(dve, it, l)
                    else:
                        D["out1" if name == "y2" else "out2"].wait(dve, it, l)
                    ins = v.tensor_tensor(y, bank[l][:, :], d[res][l], ALU.add)
                elif name == "ya":
                    D["xs2"].wait(dve, it, l)
                    ins = v.tensor_tensor(rows(y), rows(d["xs2"][l]), over_rows(bc["gb2"]), ALU.add)
                elif name == "y1":
                    D["ya"].wait(dve, it, l)
                    ins = v.scalar_tensor_tensor(y, y, 0.0, d["x1"][l], ALU.max, ALU.add)
                elif name.startswith("st"):
                    D["y" + name[2:]].wait(dve, it, l)
                    for j in range(TILES):
                        ins = v.bn_stats(st[:, l, j, :], y[:, j * P:(j + 1) * P])
                elif name.startswith("var"):
                    D["st" + name[3:]].wait(dve, it, l)
                    settle(dve, s_settle)
                    for j in range(TILES):
                        ins = v.bn_aggr(mv[:, l, j, :], st[:, l, j, :])
                elif name.startswith("rs"):
                    D["sd" + name[2:]].wait(dve, it, l)
                    ins = v.reciprocal(rs[:, l, :], sd[:, l, :])
                else:
                    n = int(name[3:])
                    D[f"rs{n}"].wait(dve, it, l)
                    if n == 1:
                        D["stored"].wait(dve, it, l)
                    for j in range(TILES):
                        ins = v.tensor_scalar(d[normed[n]][l][:, j * P:(j + 1) * P], y[:, j * P:(j + 1) * P],
                                              mv[:, l, j, 0:1], rs[:, l, j:j + 1], ALU.subtract, ALU.mult)
                ins.then_inc(D[name].sems[l], 1)

            dense_rounds(dve, "vector", step)

        def gather4(pool, stage, cols, use, it, i2, par, source, free, into=None):
            for l in range(EL):
                n = num(use, it, l)
                for f, lag in free:
                    pool.wait_ge(f.sem, f.done(n - lag))
                    settle(pool, s_dsc)
                nc.gpsimd.tensor_copy(IDX[par][l][:, :], cols[:, bass.ds(it * (EL * TILES) + l * TILES, TILES)])\
                  .then_inc(stage.sem, 1)
                pool.wait_ge(stage.sem, stage.done(n))
                settle(pool, s_dsc)
                for j in range(TILES):
                    pool.indirect_dma_start(rows((into or GG)[par][l])[:, j, :], None, source,
                                            bass.IndirectOffsetOnAxis(ap=IDX[par][l][:, j:j + 1], axis=0))\
                        .then_inc(s_gather[par][l], 16)

        GG, IDX, s_gather = (G, H), (idx, idx2), (s_ga, s_gb)

        def gathered(eng, phase, k, i2, par, l):
            before = sum(dmas("gathered", *p) for p in ORDER[:ORDER.index((phase, k))])
            eng.wait_ge(s_gather[par][l], i2 * (16 * TILES) + (16 * before * (EIT // 2) + 16 * TILES))

        def wait_chunk(eng, stage, n):
            eng.wait_ge(stage.sem, stage.done(n))

        def spread_mask(e0):
            return same[:, bass.ds(e0 + 1, CH)]

        def put_state(dve, src, it, l, signal):
            e0 = at(it, l)
            nc.vector.scalar_tensor_tensor(state[:, bass.ds(e0, CH)], spread_mask(e0), 0.0, src,
                                           ALU.is_equal, ALU.mult).then_inc(signal.sem, 1)

        TAILS = [dict(bias="b2", res=own[0], base=0, keep=(own[1], 0), mat="gS0", to=table[1]),
                 dict(bias=None, res=own[1], base=0, keep=(table[4], NP), mat=None, to=None),
                 dict(bias="l2", res=table[4], base=NP, keep=(own[5], 0), mat="V1", to=table[5]),
                 dict(bias="b3", res=own[5], base=0, keep=None, mat=None, to=None)]
        MAT_USE = {0: 0, 2: 1}
        STEPS = {0: dict(bias="gb0", mat="gS1", to=table[2]), 1: dict(bias="gb1", mat="gS2", to=table[3]),
                 2: dict(bias="gb2"), 3: dict(bias="vb1", mat="V2", to=table[6]), 4: dict(bias="vb2", mat=None, to=table[7])}
        STEP_USE = {0: 0, 1: 1, 3: 2, 4: 3}

        ORDER = [("first", 0), ("weights", 0)]
        for k in range(3):
            ORDER += [("scores2", k), ("weights", 1 + k), ("combine", k)]
        ORDER += [("mean", 0)]
        for k in range(2):
            ORDER += [("scores4", k), ("weights", 4 + k), ("combine", 3 + k)]
        ORDER += [("scores4", 2), ("weights", 6), ("heads", 0)]

        def dmas(what, phase, k):
            return {"store": {"first": 2, "scores2": 2, "scores4": 2, "combine": 1, "mean": 2},
                    "load": {"first": 1, "combine": 1, "heads": 1},
                    "load_own": {"first": 1, "combine": 2 if k == 2 else 1, "mean": 1, "heads": 1},
                    "gathered": {"scores2": TILES, "mean": TILES, "scores4": TILES}}[what].get(phase, 0)

        def landed(what, phase, k, it):
            before = sum(dmas(what, *p) for p in ORDER[:ORDER.index((phase, k))])
            per = dmas(what, phase, k)
            return it * (16 * per) + 16 * (before * EIT + per + (what == "store"))

        def rows_free(sp, phase, k, it, l):
            sp.wait_ge(s_st[l], landed("store", phase, k, it) - 16 * dmas("store", phase, k))
            settle(sp, s_sync)

        def rows_out(eng, phase, it, l):
            eng.wait_ge(s_in2[l], landed("load_own", phase, 0, it))

        def stores_landed(sp, phase, k):
            for l in range(EL):
                sp.wait_ge(s_st[l], landed("store", phase, k, EIT - 1))

        def tail_vector(dve, k, it, into, feat, new):
            for l in range(EL):
                wait_chunk(dve, TL["o"], num(k, it, l))
                dve.wait_ge(s_in2[l], landed("load_own", *TAIL_PHASE[k], it))
                if k == 1:
                    wait_chunk(dve, CA["relu"], num(2, it, l))
                if l == EL - 1:
                    last, use = {0: (E0, 0), 1: (CA, 2), 2: (CM, 0)}[k]
                    wait_chunk(dve, last["last"], use * EIT + it)
                nc.vector.tensor_tensor(into[l], bank[l][:, :], H[l], ALU.add).then_inc(TL["y"].sem, 1)
            norm_vector(dve, LNS, EL, it * EL + k * ECH, lambda l: TL["y"].done(num(k, it, l)), TL["y"].sem, into, new)
            for l in range(EL if k in MAT_USE else 0):
                wait_chunk(dve, TL["x"], num(k, it, l))
                put_state(dve, feat[l], it, l, TL["state"])

        def tail_scalar(act, k, it, feat, rows_to):
            norm_scalar(act, LNS, EL, it * EL + k * ECH)
            for l in range(EL if k < 3 else 0):
                wait_chunk(act, TL["xt"], num(k, it, l))
                to = feat[l] if feat else state[:, bass.ds(at(it, l), CH)]
                nc.scalar.activation(to, bank[l][:, :], ACT.Copy).then_inc(TL["x"].sem, 1)
            for l in range(EL if k in MAT_USE else 0):
                wait_chunk(act, TL["r"], num(MAT_USE[k], it, l))
                nc.scalar.activation(rows_to[l], bank[l][:, :], ACT.Copy).then_inc(TL["g"].sem, 1)

        def tail_tensor(pe, k, it, feat, new):
            for l in range(EL):
                wait_chunk(pe, LNS["out"], num(k, it, l))
                transpose4(new[l], bank[l]).then_inc(TL["xt"].sem, 1)
            for l in range(EL if k in MAT_USE else 0):
                wait_chunk(pe, TL["x"], num(k, it, l))
                rows4(feat[l], mats[TAILS[k]["mat"]], bank[l]).then_inc(TL["r"].sem, 1)

        def tail_sync(sp, k, it, new, rows_from):
            tl = TAILS[k]
            for l in range(EL):
                wait_chunk(sp, LNS["out"], num(k, it, l))
                settle(sp, s_sync)
                target, base = tl["keep"]
                sp.dma_start(slot_rows(target, at(it, l), base), rows(new[l])).then_inc(s_st[l], 16)
            for l in range(EL if k in MAT_USE else 0):
                wait_chunk(sp, TL["g"], num(MAT_USE[k], it, l))
                settle(sp, s_sync)
                sp.dma_start(slot_rows(tl["to"], at(it, l), NP), rows(rows_from[l])).then_inc(s_st[l], 16)

        TAIL_PHASE = [("first", 0), ("combine", 2), ("mean", 0), ("heads", 0)]


        def first_sync(sp, use):
            def load_src(it):
                for l in range(EL):
                    if not isinstance(it, int):
                        wait_chunk(sp, E0["scan"], num(0, it, l) - EL)
                        settle(sp, s_sync)
                    sp.dma_start(rows(G[l]), slot_rows(staged, at(it, l))).then_inc(s_in[l], 16)
                    sp.dma_start(ew[:, l * CH:(l + 1) * CH], a["ew"][bass.ds(at(it, l), CH)].unsqueeze(0))\
                      .then_inc(s_ew[l], 16)

            def body(it, more):
                for l in range(EL):
                    rows_free(sp, "first", 0, it, l)
                    sp.dma_start(rows(H[l]), slot_rows(own[0], at(it, l))).then_inc(s_in2[l], 16)
                if more:
                    load_src(it + 1)
                tail_sync(sp, 0, it, B, H)

            load_src(0)
            with sp.Fori(0, EIT - 1) as it:
                body(it, True)
            body(EIT - 1, False)
            stores_landed(sp, "first", 0)

        def first_pool(pool, use):
            pass

        def first_tensor(pe, use):
            t = nc.tensor
            with pe.Fori(0, EIT) as it:
                for l in range(EL):
                    pe.wait_ge(s_in[l], landed("load", "first", 0, it))
                    wait_chunk(pe, TL["g"], num(0, it, l) - EL)
                    transpose4(G[l], bank[l]).then_inc(E0["gT"].sem, 1)
                for l in range(EL):
                    pe.wait_ge(s_in2[l], landed("load_own", "first", 0, it))
                    wait_chunk(pe, E0["a"], num(0, it, l))
                    transpose4(H[l], bank[l]).then_inc(E0["hT"].sem, 1)
                for l in range(EL):
                    wait_chunk(pe, E0["s"], num(0, it, l))
                    pe.wait_ge(s_ew[l], it * 16 + 16)
                    t.matmul(bank[l][:, :], mats["Ws0"][:, :], A[l], start=True, stop=False)
                    t.matmul(bank[l][:, :], ww[:, :], ew[:, l * CH:(l + 1) * CH], start=False, stop=True)\
                     .then_inc(E0["m"].sem, 1)
                for l in range(EL):
                    wait_chunk(pe, E0["scan"], num(0, it, l))
                    t.matmul(bank[l][:, :], mats["W1b"][:, :], B[l], start=True, stop=False)
                    t.matmul(bank[l][:, :], mats["Wz"][:, :], state[:, bass.ds(at(it, l), CH)], start=False, stop=True)\
                     .then_inc(E0["h"].sem, 1)
                for l in range(EL):
                    wait_chunk(pe, E0["r"], num(0, it, l))
                    bias_rows("b2", bank[l])
                    rows4_add(A[l], mats["W2"], bank[l], True).then_inc(TL["o"].sem, 1)
                tail_tensor(pe, 0, it, A, B)

        def first_scalar(act, use):
            with act.Fori(0, EIT) as it:
                for l in range(EL):
                    wait_chunk(act, E0["gT"], num(0, it, l))
                    wait_chunk(act, TL["state"], num(0, it, l) - EL)
                    nc.scalar.activation(A[l], bank[l][:, :], ACT.Copy).then_inc(E0["a"].sem, 1)
                for l in range(EL):
                    wait_chunk(act, E0["hT"], num(0, it, l))
                    nc.scalar.activation(state[:, bass.ds(at(it, l), CH)], bank[l][:, :], ACT.Copy)\
                      .then_inc(E0["s"].sem, 1)
                for l in range(EL):
                    wait_chunk(act, E0["h"], num(0, it, l))
                    nc.scalar.activation(A[l], bank[l][:, :], ACT.Relu, bias=c["bz"][:, :]).then_inc(E0["r"].sem, 1)
                tail_scalar(act, 0, it, A, H)

        def first_vector(dve, use):
            v = nc.vector
            v.memset(carry[:, 0:1], NEG).then_inc(s_cz, 1)
            dve.wait_ge(s_cz, 1)
            with dve.Fori(0, EIT) as it:
                for l in range(EL):
                    wait_chunk(dve, E0["gT"], num(0, it, l))
                    v.tensor_scalar(G[l], same[:, bass.ds(at(it, l), CH)], -1.0, -NEG, ALU.add, ALU.mult)\
                     .then_inc(E0["neg"].sem, 1)
                for l in range(EL):
                    n = num(0, it, l)
                    wait_chunk(dve, E0["neg"], n)
                    wait_chunk(dve, E0["m"], n)
                    if l:
                        wait_chunk(dve, E0["scan"], n - 1)
                    else:
                        wait_chunk(dve, E0["last"], it - 1)
                    rows_out(dve, "first", it, l)
                    v.tensor_tensor_scan(B[l], G[l], bank[l][:, :], B[l - 1][:, CH - 1:CH] if l else carry[:, 0:1],
                                         ALU.add, ALU.max).then_inc(E0["scan"].sem, 1)
                wait_chunk(dve, E0["scan"], num(0, it, EL - 1))
                v.tensor_copy(carry[:, 0:1], B[EL - 1][:, CH - 1:CH]).then_inc(E0["last"].sem, 1)
                tail_vector(dve, 0, it, B, A, B)

        PIECE = EL * CH

        def spread_runs(dve, use):
            for i in reversed(range(EIT)):
                mask, piece = same[:, i * PIECE + 1:(i + 1) * PIECE + 1], state[:, i * PIECE:(i + 1) * PIECE]
                carry_ = 0.0 if i == EIT - 1 else carry[:, 0:1]
                dve_step = 2 * (use * EIT + EIT - 1 - i)
                nc.vector.tensor_tensor_scan(piece[:, ::-1], mask[:, ::-1], piece[:, ::-1], carry_, ALU.mult, ALU.add)\
                  .then_inc(s_spread, 1)
                dve.wait_ge(s_spread, dve_step + 1)
                nc.vector.tensor_copy(carry[:, 0:1], piece[:, 0:1]).then_inc(s_spread, 1)
                dve.wait_ge(s_spread, dve_step + 2)

        def spread_done(eng, use):
            eng.wait_ge(s_spread, 2 * EIT * (use + 1))

        def scores2_sync(sp, k):
            with sp.Fori(0, EIT // 2) as i2:
                for par in range(2):
                    it = i2 * 2 + par
                    for l in range(EL):
                        gathered(sp, "scores2", k, i2, par, l)
                        settle(sp, s_sync)
                        sp.dma_start(slot_rows(staged, at(it, l)), rows(GG[par][l])).then_inc(s_st[l], 16)
                    for l in range(EL):
                        wait_chunk(sp, GA["row"], num(k, it, l))
                        settle(sp, s_sync)
                        sp.dma_start(scores[0:1, bass.ds(at(it, l), CH)], score_rows[l][0:1, :]).then_inc(s_st[l], 16)
                    for l in range(EL):
                        sp.wait_ge(s_st[l], landed("store", "scores2", k, it))
                        sp.sem_inc(GA["stored"].sem, 1)

        def scores2_pool(pool, k):
            with pool.Fori(0, EIT // 2) as i2:
                for par in range(2):
                    it = i2 * 2 + par
                    gather4(pool, GA["idx"], gather_row, k, it, i2, par, table[1 + k], [(GA["pre"], 2 * EL), (GA["stored"], 2 * EL)])

        def scores2_tensor(pe, k):
            t = nc.tensor
            spread_done(pe, k)
            with pe.Fori(0, EIT // 2) as i2:
                for par in range(2):
                    it = i2 * 2 + par
                    for l in range(EL):
                        gathered(pe, "scores2", k, i2, par, l)
                        wait_chunk(pe, GA["row"], num(k, it, l) - EL)
                        t.matmul(bank[l][:, :], mats[f"gD{k}"][:, :], state[:, bass.ds(at(it, l), CH)], start=True, stop=False)
                        for j in range(TILES):
                            last = t.matmul(bank[l][:, j * P:(j + 1) * P], GG[par][l][:, j * P:(j + 1) * P], ident[:, :],
                                            start=False, stop=(j == TILES - 1), is_transpose=True)
                        last.then_inc(GA["pre"].sem, 1)
                    for l in range(EL):
                        wait_chunk(pe, GA["a"], num(k, it, l))
                        t.matmul(bank[l][:, :], mats[f"gB{k}"][:, :], state[:, bass.ds(at(it, l), CH)], start=True, stop=True)\
                         .then_inc(GA["self"].sem, 1)
                    for l in range(EL):
                        wait_chunk(pe, GA["la"], num(k, it, l))
                        wait_chunk(pe, GA["lb"], num(k, it, l))
                        t.matmul(bank[l][0:1, :], c[f"att{k}"][:, :], A[l], start=True, stop=False)
                        t.matmul(bank[l][0:1, :], c[f"natt{k}"][:, :], B[l], start=False, stop=True).then_inc(GA["e"].sem, 1)

        def scores2_scalar(act, k):
            with act.Fori(0, EIT // 2) as i2:
                for par in range(2):
                    it = i2 * 2 + par
                    for l in range(EL):
                        wait_chunk(act, GA["pre"], num(k, it, l))
                        nc.scalar.activation(A[l], bank[l][:, :], ACT.Copy).then_inc(GA["a"].sem, 1)
                    for l in range(EL):
                        wait_chunk(act, GA["self"], num(k, it, l))
                        nc.scalar.activation(B[l], bank[l][:, :], ACT.Copy).then_inc(GA["b"].sem, 1)
                    for l in range(EL):
                        wait_chunk(act, GA["stored"], num(k, it, l) - EL)
                        wait_chunk(act, GA["e"], num(k, it, l))
                        nc.scalar.activation(score_rows[l][0:1, :], bank[l][0:1, :], ACT.Copy).then_inc(GA["row"].sem, 1)

        def scores2_vector(dve, k):
            spread_runs(dve, k)
            with dve.Fori(0, EIT) as it:
                for ready, buf, signal in (("a", A, "la"), ("b", B, "lb")):
                    for l in range(EL):
                        wait_chunk(dve, GA[ready], num(k, it, l))
                        nc.vector.scalar_tensor_tensor(buf[l], buf[l], SLOPE, buf[l], ALU.mult, ALU.max)\
                          .then_inc(GA[signal].sem, 1)

        def scores4_sync(sp, k):
            with sp.Fori(0, EIT // 2) as i2:
                for par in range(2):
                    it = i2 * 2 + par
                    for l in range(EL):
                        gathered(sp, "scores4", k, i2, par, l)
                        settle(sp, s_sync)
                        sp.dma_start(slot_rows(staged, at(it, l)), rows(GG[par][l])).then_inc(s_st[l], 16)
                    for l in range(EL):
                        wait_chunk(sp, LA["row"], num(k, it, l))
                        settle(sp, s_sync)
                        sp.dma_start(scores[:, bass.ds(at(it, l), CH)], score_rows[l]).then_inc(s_st[l], 16)
                    for l in range(EL):
                        sp.wait_ge(s_st[l], landed("store", "scores4", k, it))
                        sp.sem_inc(LA["stored"].sem, 1)

        def scores4_pool(pool, k):
            with pool.Fori(0, EIT // 2) as i2:
                for par in range(2):
                    it = i2 * 2 + par
                    gather4(pool, LA["idx"], gather_row, k, it, i2, par, table[5 + k], [(LA["gT"], 2 * EL), (LA["stored"], 2 * EL)])

        def scores4_tensor(pe, k):
            t = nc.tensor
            spread_done(pe, 3 + k)
            with pe.Fori(0, EIT // 2) as i2:
                for par in range(2):
                    it = i2 * 2 + par
                    for l in range(EL):
                        gathered(pe, "scores4", k, i2, par, l)
                        wait_chunk(pe, LA["row"], num(k, it, l) - EL)
                        transpose4(GG[par][l], bank[l]).then_inc(LA["gT"].sem, 1)
                    for l in range(EL):
                        wait_chunk(pe, LA["a"], num(k, it, l))
                        t.matmul(bank[l][0:2 * HEADS, :], src8[k + 1][:, :], A[l], start=True, stop=False)
                        t.matmul(bank[l][0:2 * HEADS, :], dst8[k + 1][:, :], state[:, bass.ds(at(it, l), CH)],
                                 start=False, stop=True).then_inc(LA["e"].sem, 1)

        def scores4_scalar(act, k):
            with act.Fori(0, EIT // 2) as i2:
                for par in range(2):
                    it = i2 * 2 + par
                    for l in range(EL):
                        wait_chunk(act, LA["gT"], num(k, it, l))
                        nc.scalar.activation(A[l], bank[l][:, :], ACT.Copy).then_inc(LA["a"].sem, 1)
                    for l in range(EL):
                        wait_chunk(act, LA["stored"], num(k, it, l) - EL)
                        wait_chunk(act, LA["e"], num(k, it, l))
                        nc.scalar.activation(score_rows[l], bank[l][0:2 * HEADS, :], ACT.Copy)\
                          .then_inc(LA["row"].sem, 1)

        def scores4_vector(dve, k):
            spread_runs(dve, 3 + k)

        MEAN, GAT2, GAT = "mean", "gat2", "gat"
        CALLS = [(MEAN, 0, 0)] + [(GAT2, k, 0) for k in range(3)] + [(GAT, k, h) for k in range(3) for h in range(HEADS)]
        TOP = "mf mb mef meb mcar m1 m2 m3 m4 m5 dm".split()
        SUM = "sf sb sef seb scar s1 s2 s3 s4 s5 s6".split()
        VSTEPS = {MEAN: ["w"] + SUM + ["mx", "rec", "alc"],
                  GAT2: TOP + SUM + ["s7", "rec", "al", "as1", "as2", "alc", "asc"],
                  GAT: ["le", "ls", "d"] + TOP + SUM + ["s7", "rec", "al", "as1", "as2", "alc", "asc"]}
        TSTEPS = {MEAN: ["srow", "scol", "tr"]}
        TSTEPS[GAT2] = TSTEPS[GAT] = ["mrow", "mcol", "srow", "scol", "tr"]

        def step(table_, call, name):
            return sum(len(table_[kd]) for kd, _, _ in CALLS[:call]) + table_[CALLS[call][0]].index(name) + 1

        def loads_before(call):
            return 16 * sum({MEAN: 0, GAT2: 1, GAT: 2}[kd] for kd, _, _ in CALLS[:call + 1])

        def calls_of(phase_use):
            return {0: [0], 1: [1], 2: [2], 3: [3], 4: [4, 5, 6, 7], 5: [8, 9, 10, 11], 6: [12, 13, 14, 15]}[phase_use]

        def weights_sync(sp, u):
            for call in calls_of(u):
                kind, k, h = CALLS[call]
                if call != calls_of(u)[0]:
                    sp.wait_ge(s_vs, step(VSTEPS, call - 1, "d"))
                if kind != MEAN:
                    sp.dma_start(compact_sb(T["e"]), compact(scores[h, :])).then_inc(s_ds, 16)
                if kind == GAT:
                    sp.dma_start(compact_sb(T["s"]), compact(scores[HEADS + h, :])).then_inc(s_ds, 16)

        def weights_pool(pool, u):
            pass

        def weights_scalar(act, u):
            for call in calls_of(u):
                if CALLS[call][0] == MEAN:
                    continue
                act.wait_ge(s_vs, step(VSTEPS, call, "dm"))
                nc.scalar.activation(T["w"], T["dm"], ACT.Exp)
                nc.scalar.activation(T["c"], T["m"], ACT.Exp, scale=-1.0).then_inc(s_as, 1)

        def exps_before(call):
            return sum(1 for kd, _, _ in CALLS[:call + 1] if kd != MEAN)

        def weights_tensor(pe, u):
            t = nc.tensor
            for call in calls_of(u):
                kind = CALLS[call][0]
                for q in (("m", "s") if kind != MEAN else ("s",)):
                    pe.wait_ge(s_vs, step(VSTEPS, call, q + "b"))
                    for i, (m, col) in enumerate((("f", P - 1), ("f", 2 * P - 1), ("b", 0), ("b", P))):
                        last = t.transpose(bank[0][0:1, i * RP:(i + 1) * RP], T[m][:, col:col + 1], ident[0:RP, 0:RP])
                    last.then_inc(s_ts, 1)
                    pe.wait_ge(s_vs, step(VSTEPS, call, q + "eb"))
                    for i, off in enumerate((0, RP, NT + 2, NT + 2 + RP)):
                        last = t.matmul(bank[1][0:RP, i:i + 1], erow[0:1, off:off + RP], one[:, :], start=True, stop=True)
                    last.then_inc(s_ts, 1)
                pe.wait_ge(s_vs, step(VSTEPS, call, "as2" if kind != MEAN else "rec"))
                for i, m in enumerate(("t", "u") if kind != MEAN else ("t",)):
                    for g in range(2):
                        last = t.transpose(bank[2][:, i * NT + g * RP:i * NT + (g + 1) * RP], T[m][:, g * P:(g + 1) * P],
                                           ident[0:RP, 0:RP])
                last.then_inc(s_ts, 1)

        def weights_vector(dve, u):
            v = nc.vector
            for call in calls_of(u):
                kind, k, h = CALLS[call]
                names_ = VSTEPS[kind]
                at_ = [0]

                def link(name, ins):
                    assert names_[at_[0]] == name
                    at_[0] += 1
                    ins.then_inc(s_vs, 1)
                    dve.wait_ge(s_vs, step(VSTEPS, call, name))

                def halves(name, out_, flags, col, in1, op, first):
                    for g in range(2):
                        sl = slice(g * P, (g + 1) * P)
                        link(f"{name}{first + g}", v.scalar_tensor_tensor(out_[:, sl], flags[:, sl], ccol[:, col + g:col + g + 1],
                                                                          in1[:, sl], ALU.mult, op))

                def run_totals(q, x, op, total):
                    link(q + "f", v.tensor_tensor_scan(T["f"], R["contz"][:, :], x, 0.0, ALU.mult, op))
                    link(q + "b", v.tensor_tensor_scan(T["b"][:, ::-1], R["contbz"][:, ::-1], x[:, ::-1], 0.0, ALU.mult, op))
                    dve.wait_ge(s_ts, step(TSTEPS, call, q + "row"))
                    link(q + "ef", v.tensor_tensor_scan(erow[:, 1:NT + 1], frow[:, 0:NT], bank[0][0:1, 0:NT], 0.0,
                                                        ALU.mult, op))
                    link(q + "eb", v.tensor_tensor_scan(erow[:, NT + 1:2 * NT + 1][:, ::-1], frow[:, NT:][:, ::-1],
                                                        bank[0][0:1, NT:2 * NT][:, ::-1], 0.0, ALU.mult, op))
                    dve.wait_ge(s_ts, step(TSTEPS, call, q + "col"))
                    link(q + "car", v.tensor_copy(ccol[:, :], bank[1][0:RP, 0:4]))
                    halves(q, total, R["pre"], 0, T["f"], op, 1)
                    halves(q, total, R["suf"], 2, total, op, 3)
                    link(q + "5", v.tensor_tensor(total, total, T["b"], op))

                if kind == MEAN:
                    link("w", v.memset(T["w"], 1.0))
                else:
                    dve.wait_ge(s_ds, loads_before(call))
                    if kind == GAT:
                        link("le", v.scalar_tensor_tensor(T["d"], T["e"], SLOPE, T["e"], ALU.mult, ALU.max))
                        link("ls", v.scalar_tensor_tensor(T["di"], T["s"], SLOPE, T["s"], ALU.mult, ALU.max))
                        link("d", v.tensor_tensor(T["d"], T["d"], T["di"], ALU.subtract))
                        score = T["d"]
                    else:
                        score = T["e"]
                    run_totals("m", score, ALU.max, T["m"])
                    link("dm", v.tensor_tensor(T["dm"], score, T["m"], ALU.subtract))
                    dve.wait_ge(s_as, exps_before(call))
                run_totals("s", T["w"], ALU.add, T["t"])
                link("s6", v.tensor_tensor(T["t"], T["t"], T["w"], ALU.subtract))
                if kind == MEAN:
                    link("mx", v.tensor_scalar(T["t"], T["t"], 1.0, None, ALU.max))
                    link("rec", v.reciprocal(T["t"], T["t"]))
                    dve.wait_ge(s_ts, step(TSTEPS, call, "tr"))
                    link("alc", v.tensor_copy(mean_w[:, :], bank[2][:, 0:NT]))
                    continue
                link("s7", v.scalar_tensor_tensor(T["t"], T["t"], 1e-16 if kind == GAT2 else 0.0, T["c"], ALU.add, ALU.add))
                link("rec", v.reciprocal(T["u"], T["t"]))
                link("al", v.tensor_tensor(T["t"], T["w"], T["u"], ALU.mult))
                link("as1", v.tensor_tensor(T["u"], T["c"], T["u"], ALU.mult))
                link("as2", v.tensor_tensor(T["u"], T["u"], R["end"][:, :], ALU.mult))
                dve.wait_ge(s_ts, step(TSTEPS, call, "tr"))
                al_to, as_to = (alpha[:, 0:NT], aself[:, 0:NT]) if kind == GAT2 else (alpha4[:, :, h], aself4[:, :, h])
                link("alc", v.tensor_copy(al_to, bank[2][:, 0:NT]))
                link("asc", v.tensor_copy(as_to, bank[2][:, NT:2 * NT]))

        def weight_ap(w, it, l, heads):
            if heads == 1:
                return w[:, bass.ds(it * (EL * TILES) + l * TILES, TILES)].unsqueeze(2).to_broadcast([P, TILES, P])
            v4 = w[:, bass.ds(it * (EL * TILES * HEADS) + l * (TILES * HEADS), TILES * HEADS)]
            return v4.unsqueeze(2).to_broadcast([P, TILES * HEADS, P // HEADS])

        def weight_head(w, it, l, h):
            v4 = w[:, bass.ds(it * (EL * TILES * HEADS) + l * (TILES * HEADS), TILES * HEADS)]
            return v4.rearrange("p (j h) -> p j h", h=HEADS)[:, :, h].unsqueeze(2).to_broadcast([P, TILES, P])

        def split(buf, heads):
            return rows(buf) if heads == 1 else buf.rearrange("p (j f) -> p j f", j=TILES * HEADS)

        COMBINES = [(table[1], 1), (table[2], 1), (table[3], 1), (table[5], HEADS), (table[6], HEADS)]

        def combine_sync(sp, k):
            def load(it, before):
                for l in range(EL):
                    if before is not None:
                        wait_chunk(sp, CA["t"], num(k, before, l))
                        settle(sp, s_sync)
                    sp.dma_start(rows(G[l]), slot_rows(staged, at(it, l))).then_inc(s_in[l], 16)
                    if k == 2 and before is not None:
                        wait_chunk(sp, TL["y"], num(1, before, l))
                        settle(sp, s_sync)
                    sp.dma_start(rows(H[l]), slot_rows(COMBINES[k][0], at(it, l), NP)).then_inc(s_in2[l], 16)

            def body(it, more):
                if k == 2:
                    for l in range(EL):
                        wait_chunk(sp, CA["t"], num(k, it, l))
                        settle(sp, s_sync)
                        sp.dma_start(rows(H[l]), slot_rows(TAILS[1]["res"], at(it, l))).then_inc(s_in2[l], 16)
                if more:
                    load(it + 1, it)
                if k == 2:
                    tail_sync(sp, 1, it, A, None)
                else:
                    for l in range(EL):
                        wait_chunk(sp, CA["rows"], num(STEP_USE[k], it, l))
                        settle(sp, s_sync)
                        sp.dma_start(slot_rows(STEPS[k]["to"], at(it, l), NP), rows(A[l])).then_inc(s_st[l], 16)
                for l in range(EL):
                    sp.wait_ge(s_st[l], landed("store", "combine", k, it))
                    sp.sem_inc(CA["stored"].sem, 1)

            load(0, None)
            with sp.Fori(0, EIT - 1) as it:
                body(it, True)
            body(EIT - 1, False)

        def combine_pool(pool, k):
            heads = COMBINES[k][1]
            with pool.Fori(0, EIT) as it:
                for l in range(EL):
                    pool.wait_ge(s_in2[l], landed("load_own", "combine", k, it) - (16 if k == 2 else 0))
                    settle(pool, s_dsc)
                    nc.gpsimd.tensor_tensor(split(H[l], heads), split(H[l], heads), weight_ap(aself, it, l, heads), ALU.mult)\
                      .then_inc(CA["h"].sem, 1)

        def combine_vector(dve, k):
            v = nc.vector
            heads = COMBINES[k][1]
            v.memset(carry[:, 0:1], 0.0).then_inc(s_cz, 1)
            cz[0] += 1
            dve.wait_ge(s_cz, cz[0])
            with dve.Fori(0, EIT) as it:
                for l in range(EL):
                    dve.wait_ge(s_in[l], landed("load", "combine", k, it))
                    v.tensor_tensor(split(G[l], heads), split(G[l], heads), weight_ap(alpha, it, l, heads), ALU.mult)\
                     .then_inc(CA["g"].sem, 1)
                for l in range(EL):
                    if l:
                        wait_chunk(dve, CA["v"], num(k, it, l) - 1)
                    else:
                        wait_chunk(dve, CA["last"], k * EIT + it - 1)
                    wait_chunk(dve, CA["stored"], num(k, it, l) - EL)
                    wait_chunk(dve, CA["t"], num(k, it, l))
                    v.tensor_tensor_scan(A[l], same[:, bass.ds(at(it, l), CH)], bank[l][:, :],
                                         A[l - 1][:, CH - 1:CH] if l else carry[:, 0:1], ALU.mult, ALU.add)\
                     .then_inc(CA["v"].sem, 1)
                wait_chunk(dve, CA["v"], num(k, it, EL - 1))
                v.tensor_copy(carry[:, 0:1], A[EL - 1][:, CH - 1:CH]).then_inc(CA["last"].sem, 1)
                if k == 2:
                    tail_vector(dve, 1, it, A, None, A)
                else:
                    for l in range(EL):
                        wait_chunk(dve, CA["relu"], num(k, it, l))
                        put_state(dve, B[l], it, l, CA["state"])

        def wait_next_scan(eng, k, it, l):
            if l < EL - 1:
                wait_chunk(eng, CA["v"], num(k, it, l + 1))
            else:
                wait_chunk(eng, CA["last"], k * EIT + it)

        def combine_scalar(act, k):
            if k == 2:
                sqrt_table()
            with act.Fori(0, EIT) as it:
                for l in range(EL):
                    if k != 2:
                        wait_chunk(act, CA["state"], num(STEP_USE[k], it, l) - EL)
                    wait_chunk(act, CA["v"], num(k, it, l))
                    nc.scalar.activation(B[l], A[l], ACT.Relu, bias=c[STEPS[k]["bias"]][:, :]).then_inc(CA["relu"].sem, 1)
                if k == 2:
                    tail_scalar(act, 1, it, None, None)
                else:
                    for l in range(EL):
                        wait_chunk(act, CA["r"], num(STEP_USE[k], it, l))
                        wait_next_scan(act, k, it, l)
                        nc.scalar.activation(A[l], bank[l][:, :], ACT.Copy).then_inc(CA["rows"].sem, 1)

        def combine_tensor(pe, k):
            with pe.Fori(0, EIT) as it:
                for l in range(EL):
                    wait_chunk(pe, CA["g"], num(k, it, l))
                    wait_chunk(pe, CA["h"], num(k, it, l))
                    if k == 2:
                        wait_chunk(pe, TL["x"], num(1, it, l) - EL)
                    else:
                        wait_chunk(pe, CA["rows"], num(STEP_USE[k], it, l) - EL)
                    for buf in (G, H):
                        for j in range(TILES):
                            last = nc.tensor.matmul(bank[l][:, j * P:(j + 1) * P], buf[l][:, j * P:(j + 1) * P], ident[:, :],
                                                    start=(buf is G and j == 0), stop=(buf is H and j == TILES - 1),
                                                    is_transpose=True)
                    last.then_inc(CA["t"].sem, 1)
                for l in range(EL):
                    wait_chunk(pe, CA["relu"], num(k, it, l))
                    if k == 2:
                        transpose4(B[l], bank[l]).then_inc(TL["o"].sem, 1)
                    elif STEPS[k]["mat"]:
                        rows4(B[l], mats[STEPS[k]["mat"]], bank[l]).then_inc(CA["r"].sem, 1)
                    else:
                        transpose4(B[l], bank[l]).then_inc(CA["r"].sem, 1)
                if k == 2:
                    tail_tensor(pe, 1, it, None, A)

        S = [shared[:, l * CH:(l + 1) * CH] for l in range(EL)]
        GS = (G, S)

        def mean_sync(sp, k):
            with sp.Fori(0, EIT // 2) as i2:
                for par in range(2):
                    it = i2 * 2 + par
                    for l in range(EL):
                        rows_free(sp, "mean", 0, it, l)
                        sp.sem_inc(CM["stored"].sem, 1)
                        sp.dma_start(rows(H[l]), slot_rows(TAILS[2]["res"], at(it, l), TAILS[2]["base"])).then_inc(s_in2[l], 16)
                    tail_sync(sp, 2, it, GS[par], H)
            stores_landed(sp, "mean", 0)

        def mean_pool(pool, k):
            with pool.Fori(0, EIT // 2) as i2:
                for par in range(2):
                    it = i2 * 2 + par
                    gather4(pool, CM["idx"], gather_row, 0, it, i2, par, table[4], [(CM["stored"], EL)], GS)

        def mean_vector(dve, k):
            v = nc.vector
            v.memset(carry[:, 0:1], 0.0).then_inc(s_cz, 1)
            cz[0] += 1
            dve.wait_ge(s_cz, cz[0])
            with dve.Fori(0, EIT // 2) as i2:
                for par in range(2):
                    it = i2 * 2 + par
                    for l in range(EL):
                        gathered(dve, "mean", 0, i2, par, l)
                        v.tensor_tensor(rows(GS[par][l]), rows(GS[par][l]), weight_ap(mean_w, it, l, 1), ALU.mult)\
                         .then_inc(CM["g"].sem, 1)
                    for l in range(EL):
                        if l:
                            wait_chunk(dve, CM["v"], num(0, it, l) - 1)
                        else:
                            wait_chunk(dve, CM["last"], it - 1)
                        wait_chunk(dve, CM["t"], num(0, it, l))
                        v.tensor_tensor_scan(A[l], same[:, bass.ds(at(it, l), CH)], bank[l][:, :],
                                             A[l - 1][:, CH - 1:CH] if l else carry[:, 0:1], ALU.mult, ALU.add)\
                         .then_inc(CM["v"].sem, 1)
                    wait_chunk(dve, CM["v"], num(0, it, EL - 1))
                    v.tensor_copy(carry[:, 0:1], A[EL - 1][:, CH - 1:CH]).then_inc(CM["last"].sem, 1)
                    tail_vector(dve, 2, it, GS[par], B, GS[par])

        def mean_scalar(act, k):
            with act.Fori(0, EIT // 2) as i2:
                for par in range(2):
                    it = i2 * 2 + par
                    for l in range(EL):
                        wait_chunk(act, TL["r"], num(1, it, l) - EL)
                        wait_chunk(act, TL["state"], num(1, it, l) - EL)
                        nc.scalar.activation(B[l], state[:, bass.ds(at(it, l), CH)], ACT.Copy).then_inc(CM["c"].sem, 1)
                    tail_scalar(act, 2, it, B, H)

        def mean_tensor(pe, k):
            with pe.Fori(0, EIT // 2) as i2:
                for par in range(2):
                    it = i2 * 2 + par
                    for l in range(EL):
                        wait_chunk(pe, CM["g"], num(0, it, l))
                        wait_chunk(pe, TL["g"], num(1, it, l) - EL)
                        transpose4(GS[par][l], bank[l]).then_inc(CM["t"].sem, 1)
                    for l in range(EL):
                        wait_chunk(pe, CM["v"], num(0, it, l))
                        wait_chunk(pe, CM["c"], num(0, it, l))
                        bias_rows("l2", bank[l])
                        rows4_add(A[l], mats["Wa"], bank[l], False)
                        rows4_add(B[l], mats["Wx"], bank[l], True).then_inc(TL["o"].sem, 1)
                    tail_tensor(pe, 2, it, B, GS[par])

        def head_num(it, h, l):
            return it * (HEADS * EL) + (h * EL + l)

        RES, SUM_ROWS, OUT_ROWS, B2, A0, A1 = [lane_buffers(i * EL * CH, EL) for i in range(6)]
        BH, AH = (B, B2), (A0, A1)

        def heads_sync(sp, k):
            with sp.Fori(0, EIT) as it:
                for l in range(EL):
                    for stage in (C3["h"], C3["g"]):
                        wait_chunk(sp, stage, head_num(it, HEADS - 1, l) - HEADS * EL)
                        settle(sp, s_sync)
                    sp.dma_start(rows(G[l]), slot_rows(staged, at(it, l))).then_inc(s_in[l], 16)
                    sp.dma_start(rows(H[l]), slot_rows(table[7], at(it, l), NP)).then_inc(s_in2[l], 16)
                for l in range(EL):
                    wait_chunk(sp, TL["y"], num(3, it, l) - EL)
                    settle(sp, s_sync)
                    sp.dma_start(rows(RES[l]), slot_rows(TAILS[3]["res"], at(it, l))).then_inc(s_ew[l], 16)

        def heads_pool(pool, k):
            first_it = 0

            def products(it, h):
                for l in range(EL):
                    if h == 0:
                        pool.wait_ge(s_in2[l], landed("load_own", "heads", 0, it))
                        settle(pool, s_dsc)
                    wait_chunk(pool, C3["sum"], head_num(it, h, l) - 2 * EL)
                    settle(pool, s_dsc)
                    nc.gpsimd.tensor_tensor(rows(AH[h % 2][l]), rows(H[l]), weight_head(aself, it, l, h), ALU.mult)\
                      .then_inc(C3["h"].sem, 1)

            def scatter(it, l):
                if it is not first_it:
                    pool.wait_ge(s_out[l], it * (16 * TILES))
                    settle(pool, s_dsc)
                nc.gpsimd.tensor_copy(idx[l][:, :], last_row[:, bass.ds(it * (EL * TILES) + l * TILES, TILES)])\
                  .then_inc(TL["idx"].sem, 1)
                pool.wait_ge(TL["idx"].sem, TL["idx"].done(it * EL + l))
                settle(pool, s_dsc)
                wait_chunk(pool, LNS["out"], num(3, it, l))
                settle(pool, s_dsc)
                for j in range(TILES):
                    pool.indirect_dma_start(out, bass.IndirectOffsetOnAxis(ap=idx[l][:, j:j + 1], axis=0),
                                            rows(OUT_ROWS[l])[:, j, :], None, bounds_check=NP - 1,
                                            oob_is_err=False).then_inc(s_out[l], 16)

            def step_on(it):
                products(it + 1, 0)
                for h in range(1, HEADS):
                    products(it + 1, h)
                    for l in range(2 * (h - 1), min(2 * h, EL)):
                        scatter(it, l)

            for h in range(HEADS):
                products(0, h)
            step_on(first_it)
            with pool.Fori(0, EIT - 2) as i:
                step_on(i + 1)
            for l in range(EL):
                scatter(EIT - 1, l)
            for l in range(EL):
                pool.wait_ge(s_out[l], EIT * 16 * TILES)

        def heads_vector(dve, k):
            v = nc.vector
            v.memset(carry[:, :], 0.0).then_inc(s_cz, 1)
            cz[0] += 1
            dve.wait_ge(s_cz, cz[0])
            def body(it, others_before):
                for h in range(HEADS):
                    for l in range(EL):
                        n = head_num(it, h, l)
                        wait_chunk(dve, C3["g"], n)
                        wait_chunk(dve, C3["h"], n)
                        v.tensor_tensor(BH[h % 2][l], BH[h % 2][l], AH[h % 2][l], ALU.add).then_inc(C3["sum"].sem, 1)
                    for l in range(EL):
                        n = head_num(it, h, l)
                        if l:
                            wait_chunk(dve, C3["v"], n - 1)
                        else:
                            wait_chunk(dve, C3["carry"], (it - 1) * HEADS + h)
                        if l == EL - 1:
                            wait_chunk(dve, C3["carry"], it * HEADS + h - 1)
                        wait_chunk(dve, C3["z"], n - EL)
                        wait_chunk(dve, C3["t"], n)
                        v.tensor_tensor_scan(A[l], same[:, bass.ds(at(it, l), CH)], bank[l % 3][:, :],
                                             A[l - 1][:, CH - 1:CH] if l else carry[:, h:h + 1], ALU.mult, ALU.add)\
                         .then_inc(C3["v"].sem, 1)
                    wait_chunk(dve, C3["v"], head_num(it, h, EL - 1))
                    v.tensor_copy(carry[:, h:h + 1], A[EL - 1][:, CH - 1:CH]).then_inc(C3["carry"].sem, 1)
                for l in range(EL):
                    wait_chunk(dve, C3["z"], head_num(it, HEADS - 1, l))
                    dve.wait_ge(s_ew[l], it * 16 + 16 * (EIT + 1))
                    wait_chunk(dve, LNS["out"], num(3, it, l) - EL)
                    v.tensor_tensor(SUM_ROWS[l], bank[3 + l][:, :], RES[l], ALU.add).then_inc(TL["y"].sem, 1)
                for l in range(EL if others_before else 0):
                    dve.wait_ge(s_out[l], it * (16 * TILES))
                    settle(dve, s_settle)
                norm_vector(dve, LNS, EL, it * EL + 3 * ECH, lambda l: TL["y"].done(num(3, it, l)), TL["y"].sem,
                            SUM_ROWS, OUT_ROWS)

            body(0, False)
            with dve.Fori(0, EIT - 1) as i:
                body(i + 1, True)

        def heads_scalar(act, k):
            def weigh(it, h):
                for l in range(EL):
                    if h == 0:
                        act.wait_ge(s_in[l], landed("load", "heads", 0, it))
                    wait_chunk(act, C3["t"], head_num(it, h, l) - 2 * EL)
                    for j in range(TILES):
                        w = alpha[:, bass.ds(it * (EL * TILES * HEADS) + ((l * TILES + j) * HEADS + h), 1)]
                        ins = nc.scalar.activation(BH[h % 2][l][:, j * P:(j + 1) * P], G[l][:, j * P:(j + 1) * P],
                                                   ACT.Copy, scale=w)
                    ins.then_inc(C3["g"].sem, 1)

            def body(it, more):
                for h in range(HEADS):
                    if h + 1 < HEADS:
                        weigh(it, h + 1)
                    elif more:
                        weigh(it + 1, 0)
                norm_scalar(act, LNS, EL, it * EL + 3 * ECH)

            sqrt_table()
            weigh(0, 0)
            with act.Fori(0, EIT - 1) as it:
                body(it, True)
            body(EIT - 1, False)

        def heads_tensor(pe, k):
            with pe.Fori(0, EIT) as it:
                for h in range(HEADS):
                    for l in range(EL):
                        n = head_num(it, h, l)
                        wait_chunk(pe, C3["sum"], n)
                        wait_chunk(pe, C3["v"], n - 2)
                        transpose4(BH[h % 2][l], bank[l % 3]).then_inc(C3["t"].sem, 1)
                    for l in range(EL):
                        n = head_num(it, h, l)
                        wait_chunk(pe, C3["v"], n)
                        if h == 0:
                            wait_chunk(pe, TL["y"], num(3, it, l) - EL)
                            bias_rows("b3", bank[3 + l])
                        rows4_add(A[l], mats[f"q{h}"], bank[3 + l], h == HEADS - 1).then_inc(C3["z"].sem, 1)

        cz = [1]

        @block.sync
        def _(sp):
            setup_sync(sp)
            end_phase(sp)
            dense_sync(sp)
            end_phase(sp)
            run = dict(first=first_sync, scores2=scores2_sync, scores4=scores4_sync,
                       weights=weights_sync, combine=combine_sync, mean=mean_sync, heads=heads_sync)
            for i, (phase, k) in enumerate(ORDER):
                run[phase](sp, k)
                end_phase(sp, i == len(ORDER) - 1)

        @block.gpsimd
        def _(pool):
            setup_pool(pool)
            end_phase(pool)
            map_pool(pool)
            end_phase(pool)
            run = dict(first=first_pool, scores2=scores2_pool, scores4=scores4_pool,
                       weights=weights_pool, combine=combine_pool, mean=mean_pool, heads=heads_pool)
            for i, (phase, k) in enumerate(ORDER):
                run[phase](pool, k)
                end_phase(pool, i == len(ORDER) - 1)

        @block.scalar
        def _(act):
            setup_scalar(act)
            end_phase(act)
            dense_scalar(act)
            end_phase(act)
            run = dict(first=first_scalar, scores2=scores2_scalar,
                       scores4=scores4_scalar, weights=weights_scalar, combine=combine_scalar, mean=mean_scalar,
                       heads=heads_scalar)
            for i, (phase, k) in enumerate(ORDER):
                run[phase](act, k)
                end_phase(act, i == len(ORDER) - 1)

        @block.vector
        def _(dve):
            setup_vector(dve)
            end_phase(dve)
            dense_vector(dve)
            end_phase(dve)
            run = dict(first=first_vector, scores2=scores2_vector,
                       scores4=scores4_vector, weights=weights_vector, combine=combine_vector, mean=mean_vector,
                       heads=heads_vector)
            for i, (phase, k) in enumerate(ORDER):
                run[phase](dve, k)
                end_phase(dve, i == len(ORDER) - 1)

        @block.tensor
        def _(pe):
            setup_tensor(pe)
            end_phase(pe)
            dense_tensor(pe)
            end_phase(pe)
            run = dict(first=first_tensor, scores2=scores2_tensor,
                       scores4=scores4_tensor, weights=weights_tensor, combine=combine_tensor, mean=mean_tensor,
                       heads=heads_tensor)
            for i, (phase, k) in enumerate(ORDER):
                run[phase](pe, k)
                end_phase(pe, i == len(ORDER) - 1)


_WEIGHTS = ["L0_gnn_Wm", "L0_gnn_bm", "L0_gnn_W1", "L0_gnn_b1", "L0_gnn_W2", "L0_gnn_b2", "L1_gnn_W_src", "L1_gnn_W_dst",
            "L1_gnn_att", "L1_gnn_bias", "L2_gnn_weight", "L2_gnn_bias", "L3_gnn_W1", "L3_gnn_as1", "L3_gnn_ad1",
            "L3_gnn_b1", "L3_gnn_W2", "L3_gnn_as2", "L3_gnn_ad2", "L3_gnn_b2", "L3_gnn_W3", "L3_gnn_as3", "L3_gnn_ad3",
            "L3_gnn_b3"]


def kernel(**inputs):
    import numpy as _np
    import concourse.bacc as _bacc
    from concourse.bass_utils import run_bass_kernel_spmd as _run

    nc = _bacc.Bacc("TRN2", target_bir_lowering=False, num_devices=1)
    x = _np.zeros((NP + DL * CH, P), _np.float32)
    x[:N] = inputs["x"]
    src = _np.zeros(EP, _np.int32)
    src[:E] = inputs["src"]
    dst_all = _np.full(EP + 2, N, _np.int32)
    dst_all[0], dst_all[EP + 1] = -1, -1
    dst_all[1:E + 1] = inputs["dst"]
    ew = _np.zeros(EP, _np.float32)
    ew[:E] = inputs["edge_weight"]

    def by_tile(v):
        return _np.ascontiguousarray(v.reshape(NT, P).T)

    arrays = {"x": x, "src_col": by_tile(src), "dst_col": by_tile(dst_all[1:EP + 1]), "nxt_col": by_tile(dst_all[2:]),
              "dst_all": dst_all, "ew": ew}
    for name in _WEIGHTS:
        arrays[name] = _np.ascontiguousarray(inputs[name])
    args = {k: nc.dram_tensor("in_" + k, v.shape, mybir.dt.from_np(v.dtype), kind="ExternalInput").ap()
            for k, v in arrays.items()}
    out = nc.dram_tensor("out_0", (NP, P), F32, kind="ExternalOutput").ap()
    build(nc, args, out)
    r = _run(nc, [{"in_" + k: v for k, v in arrays.items()}], core_ids=[0])
    return r.results[0]["out_0"][:N]
```
